# Optimizing a Trainium2 kernel written in Bass

```python
import numpy as np
import jax
import jax.numpy as jnp

def _softmax(x, axis=-1):
    return jax.nn.softmax(x, axis=axis)

def _gelu(x):
    return jax.nn.gelu(x, approximate=True)

def _silu(x):
    return jax.nn.silu(x)

def _sigmoid(x):
    return jax.nn.sigmoid(x)

def _layernorm(x, axis=-1, eps=1e-05):
    m = jnp.mean(x, axis=axis, keepdims=True)
    v = jnp.var(x, axis=axis, keepdims=True)
    return (x - m) / jnp.sqrt(v + eps)

def _scatter_add(tgt, idx, src, axis=0):
    return tgt.at[idx].add(src)

def _segment_sum(src, seg, n):
    return jax.ops.segment_sum(src, seg, n)
kernel_name = 'mk_xattn_seq_d4_seqx_r4_5f992f'

def setup_inputs(seed: int=0):
    np.random.seed(seed)
    _w = jnp.asarray

    def _rec_inputs():
        import jax
        import jax.numpy as jnp
        _rk = jax.random.key(seed)
        x = 7.22e-05 + 1 * jax.random.normal(jax.random.fold_in(_rk, 1), (16, 256, 256), jnp.float32)
        _lenS = 256 - jax.random.randint(jax.random.fold_in(_rk, 7), (16,), 0, max(1, 256 // 4) + 1, jnp.int32)
        _lenS2 = 77 - jax.random.randint(jax.random.fold_in(_rk, 8), (16,), 0, max(1, 77 // 4) + 1, jnp.int32)
        _ctx_2048P = jax.random.normal(jax.random.fold_in(_rk, 11), (16, 16, 512), jnp.float32)
        _ctx_2048c = jax.random.dirichlet(jax.random.fold_in(_rk, 511), 0.3 * jnp.ones((16,), jnp.float32), (16, 77))
        _ctx_2048t = jnp.einsum('bsk,bkd->bsd', _ctx_2048c, _ctx_2048P)
        _ctx_2048t = _ctx_2048t * jax.lax.rsqrt(jnp.mean(jnp.square(_ctx_2048t)) + 1e-12) * 0.953939
        ctx_2048 = -1.39393e-06 + 0.999914 * (_ctx_2048t + 0.3 * jax.random.normal(jax.random.fold_in(_rk, 611), (16, 77, 512), jnp.float32))
        _validS = jnp.arange(256)[None, :] < _lenS[:, None]
        _validS2 = jnp.arange(77)[None, :] < _lenS2[:, None]
        _causal = jnp.tril(jnp.ones((256, 256), dtype=bool))
        mask_S_fk1 = jnp.where(_validS[0], 1.0, 0.0).astype(jnp.float32)
        mask_S_fk0 = jnp.where(_validS[0], 0.0, 1.0).astype(jnp.float32)
        return (x, ctx_2048, mask_S_fk1, mask_S_fk0)
    x, ctx_2048, mask_S_fk1, mask_S_fk0 = _rec_inputs()

    def _L0_xattn_setup():
        import jax, jax.numpy as jnp
        import numpy as np
        D_MODEL = 256
        N_HEADS = 16
        N_KV_HEADS = 4
        HEAD_DIM = D_MODEL // N_HEADS
        SPEAKER_DIM = 512
        EPS = 1e-05

        def rmsnorm(x, w, eps=EPS):
            xf = x.astype(jnp.float32)
            inv = jax.lax.rsqrt(jnp.mean(xf * xf, axis=-1, keepdims=True) + eps)
            return (xf * inv).astype(x.dtype) * w
        key = jax.random.key(seed)
        ks = jax.random.split(key, 7)
        B, T, S = (4, 512, 128)
        x = jax.random.normal(ks[0], (B, T, D_MODEL), dtype=jnp.float32)
        cond = jax.random.normal(ks[1], (B, S, SPEAKER_DIM), dtype=jnp.float32)
        sq = 0.02
        wq = jax.random.normal(ks[2], (D_MODEL, N_HEADS * HEAD_DIM), dtype=jnp.float32) * sq
        wk = jax.random.normal(ks[3], (SPEAKER_DIM, N_KV_HEADS * HEAD_DIM), dtype=jnp.float32) * sq
        wv = jax.random.normal(ks[4], (SPEAKER_DIM, N_KV_HEADS * HEAD_DIM), dtype=jnp.float32) * sq
        wo = jax.random.normal(ks[5], (N_HEADS * HEAD_DIM, D_MODEL), dtype=jnp.float32) * sq
        norm_w = jnp.ones((D_MODEL,), dtype=jnp.float32)
        return {'x': x, 'cond': cond, 'wq': wq, 'wk': wk, 'wv': wv, 'wo': wo, 'norm_w': norm_w}
    _L0_xattn_all = _L0_xattn_setup()
    _L0_xattn_in = {k: v for k, v in _L0_xattn_all.items() if k in ('wq', 'wk', 'wv', 'wo', 'norm_w')}
    del _L0_xattn_all

    def _L1_xattn_setup():
        import jax, jax.numpy as jnp
        import numpy as np
        HEADS = 16
        HEAD_DIM = 64
        SUPPRESS = 20.0
        key = jax.random.key(seed)
        ks = jax.random.split(key, 8)
        B, HW, C, T, CT = (8, 1024, 256, 77, 512)
        inner = HEADS * HEAD_DIM
        scale = 0.02
        return {'hidden_states': jax.random.normal(ks[0], (B, HW, C), jnp.float32), 'encoder_hidden_states': jax.random.normal(ks[1], (B, T, CT), jnp.float32), 'mask_A': (jax.random.uniform(ks[2], (HW,)) > 0.5).astype(jnp.float32), 'mask_B': (jax.random.uniform(ks[3], (HW,)) > 0.5).astype(jnp.float32), 'Wq': jax.random.normal(ks[4], (C, inner), jnp.float32) * scale, 'Wk': jax.random.normal(ks[5], (CT, inner), jnp.float32) * scale, 'Wv': jax.random.normal(ks[6], (CT, inner), jnp.float32) * scale, 'Wo': jax.random.normal(ks[7], (inner, C), jnp.float32) * scale, 'bo': jnp.zeros((C,), jnp.float32), 'token_indices_A': jnp.array([2, 3], dtype=jnp.int64), 'token_indices_B': jnp.array([5, 6], dtype=jnp.int64)}
    _L1_xattn_all = _L1_xattn_setup()
    _L1_xattn_in = {k: v for k, v in _L1_xattn_all.items() if k in ('Wq', 'Wk', 'Wv', 'Wo', 'bo', 'token_indices_A', 'token_indices_B')}
    del _L1_xattn_all

    def _L2_xattn_setup():
        import jax, jax.numpy as jnp
        import numpy as np
        HEADS = 16
        HEAD_DIM = 64
        SUPPRESS = 20.0
        key = jax.random.key(seed)
        ks = jax.random.split(key, 8)
        B, HW, C, T, CT = (8, 1024, 256, 77, 512)
        inner = HEADS * HEAD_DIM
        scale = 0.02
        return {'hidden_states': jax.random.normal(ks[0], (B, HW, C), jnp.float32), 'encoder_hidden_states': jax.random.normal(ks[1], (B, T, CT), jnp.float32), 'mask_A': (jax.random.uniform(ks[2], (HW,)) > 0.5).astype(jnp.float32), 'mask_B': (jax.random.uniform(ks[3], (HW,)) > 0.5).astype(jnp.float32), 'Wq': jax.random.normal(ks[4], (C, inner), jnp.float32) * scale, 'Wk': jax.random.normal(ks[5], (CT, inner), jnp.float32) * scale, 'Wv': jax.random.normal(ks[6], (CT, inner), jnp.float32) * scale, 'Wo': jax.random.normal(ks[7], (inner, C), jnp.float32) * scale, 'bo': jnp.zeros((C,), jnp.float32), 'token_indices_A': jnp.array([2, 3], dtype=jnp.int64), 'token_indices_B': jnp.array([5, 6], dtype=jnp.int64)}
    _L2_xattn_all = _L2_xattn_setup()
    _L2_xattn_in = {k: v for k, v in _L2_xattn_all.items() if k in ('Wq', 'Wk', 'Wv', 'Wo', 'bo', 'token_indices_A', 'token_indices_B')}
    del _L2_xattn_all

    def _L3_xattn_setup():
        import jax, jax.numpy as jnp
        import numpy as np
        HEADS = 16
        HEAD_DIM = 64
        SUPPRESS = 20.0
        key = jax.random.key(seed)
        ks = jax.random.split(key, 8)
        B, HW, C, T, CT = (8, 1024, 256, 77, 512)
        inner = HEADS * HEAD_DIM
        scale = 0.02
        return {'hidden_states': jax.random.normal(ks[0], (B, HW, C), jnp.float32), 'encoder_hidden_states': jax.random.normal(ks[1], (B, T, CT), jnp.float32), 'mask_A': (jax.random.uniform(ks[2], (HW,)) > 0.5).astype(jnp.float32), 'mask_B': (jax.random.uniform(ks[3], (HW,)) > 0.5).astype(jnp.float32), 'Wq': jax.random.normal(ks[4], (C, inner), jnp.float32) * scale, 'Wk': jax.random.normal(ks[5], (CT, inner), jnp.float32) * scale, 'Wv': jax.random.normal(ks[6], (CT, inner), jnp.float32) * scale, 'Wo': jax.random.normal(ks[7], (inner, C), jnp.float32) * scale, 'bo': jnp.zeros((C,), jnp.float32), 'token_indices_A': jnp.array([2, 3], dtype=jnp.int64), 'token_indices_B': jnp.array([5, 6], dtype=jnp.int64)}
    _L3_xattn_all = _L3_xattn_setup()
    _L3_xattn_in = {k: v for k, v in _L3_xattn_all.items() if k in ('Wq', 'Wk', 'Wv', 'Wo', 'bo', 'token_indices_A', 'token_indices_B')}
    del _L3_xattn_all
    return {'x': x, 'ctx_2048': ctx_2048, 'mask_S_fk1': mask_S_fk1, 'mask_S_fk0': mask_S_fk0, 'L0_xattn_wq': _L0_xattn_in['wq'], 'L0_xattn_wk': _L0_xattn_in['wk'], 'L0_xattn_wv': _L0_xattn_in['wv'], 'L0_xattn_wo': _L0_xattn_in['wo'], 'L0_xattn_norm_w': _L0_xattn_in['norm_w'], 'L1_xattn_Wq': _L1_xattn_in['Wq'], 'L1_xattn_Wk': _L1_xattn_in['Wk'], 'L1_xattn_Wv': _L1_xattn_in['Wv'], 'L1_xattn_Wo': _L1_xattn_in['Wo'], 'L1_xattn_bo': _L1_xattn_in['bo'], 'L1_xattn_token_indices_A': _L1_xattn_in['token_indices_A'], 'L1_xattn_token_indices_B': _L1_xattn_in['token_indices_B'], 'L2_xattn_Wq': _L2_xattn_in['Wq'], 'L2_xattn_Wk': _L2_xattn_in['Wk'], 'L2_xattn_Wv': _L2_xattn_in['Wv'], 'L2_xattn_Wo': _L2_xattn_in['Wo'], 'L2_xattn_bo': _L2_xattn_in['bo'], 'L2_xattn_token_indices_A': _L2_xattn_in['token_indices_A'], 'L2_xattn_token_indices_B': _L2_xattn_in['token_indices_B'], 'L3_xattn_Wq': _L3_xattn_in['Wq'], 'L3_xattn_Wk': _L3_xattn_in['Wk'], 'L3_xattn_Wv': _L3_xattn_in['Wv'], 'L3_xattn_Wo': _L3_xattn_in['Wo'], 'L3_xattn_bo': _L3_xattn_in['bo'], 'L3_xattn_token_indices_A': _L3_xattn_in['token_indices_A'], 'L3_xattn_token_indices_B': _L3_xattn_in['token_indices_B']}

def reference(x, ctx_2048, mask_S_fk1, mask_S_fk0, L0_xattn_wq, L0_xattn_wk, L0_xattn_wv, L0_xattn_wo, L0_xattn_norm_w, L1_xattn_Wq, L1_xattn_Wk, L1_xattn_Wv, L1_xattn_Wo, L1_xattn_bo, L1_xattn_token_indices_A, L1_xattn_token_indices_B, L2_xattn_Wq, L2_xattn_Wk, L2_xattn_Wv, L2_xattn_Wo, L2_xattn_bo, L2_xattn_token_indices_A, L2_xattn_token_indices_B, L3_xattn_Wq, L3_xattn_Wk, L3_xattn_Wv, L3_xattn_Wo, L3_xattn_bo, L3_xattn_token_indices_A, L3_xattn_token_indices_B):
    import jax
    import jax.numpy as jnp

    def _L0_xattn_ref(x, cond, wq, wk, wv, wo, norm_w):
        import jax, jax.numpy as jnp
        import numpy as np
        D_MODEL = 256
        N_HEADS = 16
        N_KV_HEADS = 4
        HEAD_DIM = D_MODEL // N_HEADS
        SPEAKER_DIM = 512
        EPS = 1e-05

        def rmsnorm(x, w, eps=EPS):
            xf = x.astype(jnp.float32)
            inv = jax.lax.rsqrt(jnp.mean(xf * xf, axis=-1, keepdims=True) + eps)
            return (xf * inv).astype(x.dtype) * w
        B, T, _ = x.shape
        S = cond.shape[1]
        n_rep = N_HEADS // N_KV_HEADS
        residual = x
        xn = rmsnorm(x, norm_w)
        q = (xn @ wq).reshape(B, T, N_HEADS, HEAD_DIM)
        k = (cond @ wk).reshape(B, S, N_KV_HEADS, HEAD_DIM)
        v = (cond @ wv).reshape(B, S, N_KV_HEADS, HEAD_DIM)
        qg = q.reshape(B, T, N_KV_HEADS, n_rep, HEAD_DIM)
        scale = 1.0 / np.sqrt(HEAD_DIM).astype(np.float32)
        scores = jnp.einsum('btgrd,bsgd->bgrts', qg, k) * scale
        attn = jax.nn.softmax(scores.astype(jnp.float32), axis=-1).astype(q.dtype)
        out = jnp.einsum('bgrts,bsgd->btgrd', attn, v).reshape(B, T, N_HEADS * HEAD_DIM)
        return residual + out @ wo

    def _L1_xattn_ref(hidden_states, encoder_hidden_states, mask_A, mask_B, Wq, Wk, Wv, Wo, bo, token_indices_A, token_indices_B):
        import jax, jax.numpy as jnp
        import numpy as np
        HEADS = 16
        HEAD_DIM = 64
        SUPPRESS = 20.0
        B, HW, C = hidden_states.shape
        T = encoder_hidden_states.shape[1]
        residual = hidden_states
        q = hidden_states @ Wq
        k = encoder_hidden_states @ Wk
        v = encoder_hidden_states @ Wv
        q = q.reshape(B, HW, HEADS, HEAD_DIM).transpose(0, 2, 1, 3)
        k = k.reshape(B, T, HEADS, HEAD_DIM).transpose(0, 2, 1, 3)
        v = v.reshape(B, T, HEADS, HEAD_DIM).transpose(0, 2, 1, 3)
        scale = HEAD_DIM ** (-0.5)
        logits = jnp.einsum('bhqd,bhkd->bhqk', q, k) * scale
        suppress_A_in = 1.0 - mask_A
        suppress_B_in = 1.0 - mask_B
        col_bias = jnp.zeros((HW, T), logits.dtype)
        col_bias = col_bias.at[:, token_indices_A].set((-SUPPRESS * suppress_A_in)[:, None])
        col_bias = col_bias.at[:, token_indices_B].set((-SUPPRESS * suppress_B_in)[:, None])
        logits = logits + col_bias[None, None, :, :]
        probs = jax.nn.softmax(logits, axis=-1)
        out = jnp.einsum('bhqk,bhkd->bhqd', probs, v)
        out = out.transpose(0, 2, 1, 3).reshape(B, HW, HEADS * HEAD_DIM)
        out = out @ Wo + bo
        out = out + residual
        return out

    def _L2_xattn_ref(hidden_states, encoder_hidden_states, mask_A, mask_B, Wq, Wk, Wv, Wo, bo, token_indices_A, token_indices_B):
        import jax, jax.numpy as jnp
        import numpy as np
        HEADS = 16
        HEAD_DIM = 64
        SUPPRESS = 20.0
        B, HW, C = hidden_states.shape
        T = encoder_hidden_states.shape[1]
        residual = hidden_states
        q = hidden_states @ Wq
        k = encoder_hidden_states @ Wk
        v = encoder_hidden_states @ Wv
        q = q.reshape(B, HW, HEADS, HEAD_DIM).transpose(0, 2, 1, 3)
        k = k.reshape(B, T, HEADS, HEAD_DIM).transpose(0, 2, 1, 3)
        v = v.reshape(B, T, HEADS, HEAD_DIM).transpose(0, 2, 1, 3)
        scale = HEAD_DIM ** (-0.5)
        logits = jnp.einsum('bhqd,bhkd->bhqk', q, k) * scale
        suppress_A_in = 1.0 - mask_A
        suppress_B_in = 1.0 - mask_B
        col_bias = jnp.zeros((HW, T), logits.dtype)
        col_bias = col_bias.at[:, token_indices_A].set((-SUPPRESS * suppress_A_in)[:, None])
        col_bias = col_bias.at[:, token_indices_B].set((-SUPPRESS * suppress_B_in)[:, None])
        logits = logits + col_bias[None, None, :, :]
        probs = jax.nn.softmax(logits, axis=-1)
        out = jnp.einsum('bhqk,bhkd->bhqd', probs, v)
        out = out.transpose(0, 2, 1, 3).reshape(B, HW, HEADS * HEAD_DIM)
        out = out @ Wo + bo
        out = out + residual
        return out

    def _L3_xattn_ref(hidden_states, encoder_hidden_states, mask_A, mask_B, Wq, Wk, Wv, Wo, bo, token_indices_A, token_indices_B):
        import jax, jax.numpy as jnp
        import numpy as np
        HEADS = 16
        HEAD_DIM = 64
        SUPPRESS = 20.0
        B, HW, C = hidden_states.shape
        T = encoder_hidden_states.shape[1]
        residual = hidden_states
        q = hidden_states @ Wq
        k = encoder_hidden_states @ Wk
        v = encoder_hidden_states @ Wv
        q = q.reshape(B, HW, HEADS, HEAD_DIM).transpose(0, 2, 1, 3)
        k = k.reshape(B, T, HEADS, HEAD_DIM).transpose(0, 2, 1, 3)
        v = v.reshape(B, T, HEADS, HEAD_DIM).transpose(0, 2, 1, 3)
        scale = HEAD_DIM ** (-0.5)
        logits = jnp.einsum('bhqd,bhkd->bhqk', q, k) * scale
        suppress_A_in = 1.0 - mask_A
        suppress_B_in = 1.0 - mask_B
        col_bias = jnp.zeros((HW, T), logits.dtype)
        col_bias = col_bias.at[:, token_indices_A].set((-SUPPRESS * suppress_A_in)[:, None])
        col_bias = col_bias.at[:, token_indices_B].set((-SUPPRESS * suppress_B_in)[:, None])
        logits = logits + col_bias[None, None, :, :]
        probs = jax.nn.softmax(logits, axis=-1)
        out = jnp.einsum('bhqk,bhkd->bhqd', probs, v)
        out = out.transpose(0, 2, 1, 3).reshape(B, HW, HEADS * HEAD_DIM)
        out = out @ Wo + bo
        out = out + residual
        return out
    x = _L0_xattn_ref(x, ctx_2048, L0_xattn_wq, L0_xattn_wk, L0_xattn_wv, L0_xattn_wo, L0_xattn_norm_w)
    x = _L1_xattn_ref(x, ctx_2048, mask_S_fk1, mask_S_fk0, L1_xattn_Wq, L1_xattn_Wk, L1_xattn_Wv, L1_xattn_Wo, L1_xattn_bo, L1_xattn_token_indices_A, L1_xattn_token_indices_B)
    x = _L2_xattn_ref(x, ctx_2048, mask_S_fk1, mask_S_fk0, L2_xattn_Wq, L2_xattn_Wk, L2_xattn_Wv, L2_xattn_Wo, L2_xattn_bo, L2_xattn_token_indices_A, L2_xattn_token_indices_B)
    x = _L3_xattn_ref(x, ctx_2048, mask_S_fk1, mask_S_fk0, L3_xattn_Wq, L3_xattn_Wk, L3_xattn_Wv, L3_xattn_Wo, L3_xattn_bo, L3_xattn_token_indices_A, L3_xattn_token_indices_B)
    return x

_drawn_inputs = setup_inputs


def setup_inputs(seed=0):
    import zlib

    import numpy as np

    out = dict(_drawn_inputs(seed))
    spreads = {'L0_xattn_norm_w': (1.0, 0.6),
     'L1_xattn_bo': (0.0, 0.1),
     'L2_xattn_bo': (0.0, 0.1),
     'L3_xattn_bo': (0.0, 0.1)}
    factors = {'mask_S_fk1': 8.0,
     'mask_S_fk0': 8.0,
     'L0_xattn_wq': 8.0,
     'L0_xattn_wk': 8.0,
     'L1_xattn_Wq': 7.706,
     'L1_xattn_Wk': 7.686,
     'L2_xattn_Wq': 7.581,
     'L2_xattn_Wk': 7.566,
     'L3_xattn_Wq': 7.312,
     'L3_xattn_Wk': 7.288}
    for name, (base, spread) in spreads.items():
        noise = np.random.default_rng([zlib.crc32(name.encode()), seed]).standard_normal(out[name].shape)
        drawn = base * np.exp(spread * noise) if base else spread * noise
        out[name] = jnp.asarray(drawn.astype(out[name].dtype))
    for name, factor in factors.items():
        out[name] = (out[name] * factor).astype(out[name].dtype)
    return out
```

```python
from contextlib import ExitStack

import concourse.bass as bass
from concourse import mybir

F32 = mybir.dt.float32
F32R = mybir.dt.float32r
I32 = mybir.dt.int32
ALU = mybir.AluOpType
ACT = mybir.ActivationFunctionType
AX = mybir.AxisListType

P = 128
LAYERS = 4
B, SQ, C = 16, 256, 256
SK, E = 77, 512
HEADS, HD = 16, 64
HD0, KVH0 = 16, 4
REP0 = HEADS // KVH0
CT, ET, QT = C // P, E // P, SQ // P
GB = 4
GROUPS = B // GB
GK, GQ = GB * SK, GB * SQ
HH = HEADS // 2
FLAT = HH * SK
HFLAT = FLAT // 2
FT = (FLAT + P - 1) // P
LAST = FLAT - (FT - 1) * P
HALVES = LAYERS * 2
UNITS = HALVES * GROUPS
ITEMS = GB * QT
MT = HEADS * HD // P
HMT = MT // 2
MATS = 2 * (LAYERS - 1)
N_G = HH * CT
N_U = GB * FT
STAGE = 2 * N_G + N_U
RCH = 512
EPS = 1e-5
SUPPRESS = 20.0
SCALE = HD ** -0.5
SCALE0 = HD0 ** -0.5
KV0_DMAS = KVH0 * 2 * REP0


def rows_of(t):
    return LAST if t == FT - 1 else P


def build(nc, xT, ctxT, wkv0, wkv, wheads, normw, bo, masks, tokens, outT):
    kv_dram = nc.dram_tensor("kv_dram", (UNITS, 2, P, HH * GK), F32, kind="Internal").ap()
    base_dram = nc.dram_tensor("base_dram", (UNITS, C, GQ), F32, kind="Internal").ap()
    query_dram = nc.dram_tensor("query_dram", (UNITS, C, GQ), F32, kind="Internal").ap()
    w_dram = nc.dram_tensor("w_dram", (HALVES, 2, HD, HH * C), F32, kind="Internal").ap()

    with ExitStack() as whole:
        def sb(name, shape, dt):
            return whole.enter_context(nc.sbuf_tensor(name, shape, dt))

        def sem(name):
            return whole.enter_context(nc.semaphore(name))

        ident = sb("ident", [P, P], F32)
        bo_sb = sb("bo_sb", [P, HALVES, CT], F32)
        key_is = sb("key_is", [4, LAYERS, GK], F32R)
        penalty = sb("penalty", [4, SQ], F32R)
        stored = [sem(f"stored{b}") for b in range(GB)]
        with ExitStack() as part:
            prepare(nc, part, xT, ctxT, wkv0, wkv, wheads, normw, bo, masks, tokens,
                    kv_dram, base_dram, query_dram, w_dram, ident, bo_sb, key_is, penalty, stored)
        with ExitStack() as part:
            attend(nc, part, kv_dram, base_dram, query_dram, w_dram,
                   ident, bo_sb, key_is, penalty, stored, outT)


def prepare(nc, ctx, xT, ctxT, wkv0, wkv, wheads, normw, bo, masks, tokens,
            kv_dram, base_dram, query_dram, w_dram, ident, bo_sb, key_is, penalty, stored):
    def sb(name, shape, dt):
        return ctx.enter_context(nc.sbuf_tensor(name, shape, dt))

    def sem(name):
        return ctx.enter_context(nc.semaphore(name))

    ctx_raw = sb("ctx_raw", [P, ET, B * SK], F32)
    ctx_hi = sb("ctx_hi", [P, ET, B * SK], F32R)
    ctx_lo = sb("ctx_lo", [P, ET, B * SK], F32R)
    w0_raw = sb("w0_raw", [P, ET, P], F32)
    w0_hi = sb("w0_hi", [P, ET, P], F32R)
    w0_lo = sb("w0_lo", [P, ET, P], F32R)
    w_raw = sb("w_raw", [P, ET, MT * P], F32)
    w_hi = [sb(f"w_hi{m}", [P, ET, MT * P], F32R) for m in range(2)]
    w_lo = [sb(f"w_lo{m}", [P, ET, MT * P], F32R) for m in range(2)]
    kv_hi = sb("kv_hi", [P, 2, HMT, GK], F32R)
    kv_lo = sb("kv_lo", [P, 2, HMT, GK], F32R)
    xr = [sb(f"xr{k}", [P, CT, RCH], F32) for k in range(2)]
    xsq = sb("xsq", [P, CT, RCH], F32)
    ms = sb("ms", [P, RCH], F32)
    root = sb("root", [P, RCH], F32)
    inv = sb("inv", [P, RCH], F32)
    corr = sb("corr", [P, RCH], F32)
    inv2 = sb("inv2", [P, RCH], F32)
    ones = sb("ones", [P, P], F32)
    nw = sb("nw", [P, CT], F32)
    nw2 = sb("nw2", [P, CT], F32)
    tok = sb("tok", [4, (LAYERS - 1) * 4], I32)
    tokf = sb("tokf", [4, (LAYERS - 1) * 4], F32)
    wrap = sb("wrap", [4, (LAYERS - 1) * 4], F32)
    keyno = sb("keyno", [4, SK], F32)
    rowno = sb("rowno", [4, 1], F32)
    sel = sb("sel", [4, 8], F32)
    is_a = sb("is_a", [4, SK], F32)
    is_b = sb("is_b", [4, SK], F32)
    other = sb("other", [4, SK], F32)
    mrow = sb("mrow", [4, SQ], F32)
    mhi = sb("mhi", [4, SQ], F32R)
    mlo = sb("mlo", [4, SQ], F32)
    ps = ctx.enter_context(nc.psum_tensor("proj_ps", [P, 8, 512], F32))

    small_in = sem("small_in")
    ctx_in = sem("ctx_in")
    w0_in = sem("w0_in")
    w_in = sem("w_in")
    w_copied = sem("w_copied")
    xr_in = [sem(f"xr_in{k}") for k in range(2)]
    xn_out = [sem(f"xn_out{k}") for k in range(2)]
    kv_out = [sem(f"kv_out{h}") for h in range(2)]
    consts = sem("consts")
    ctx_hi_done = sem("ctx_hi_done")
    ctx_lo_done = sem("ctx_lo_done")
    w0_hi_done = sem("w0_hi_done")
    w_hi_done = sem("w_hi_done")
    w_lo_done = sem("w_lo_done")
    squared = sem("squared")
    summed = sem("summed")
    ms_done = sem("ms_done")
    rooted = sem("rooted")
    xn_done = sem("xn_done")
    projected = sem("projected")
    hi_done = sem("hi_done")
    lo_done = sem("lo_done")
    dve_step = sem("dve_step")

    x_v = xT.rearrange("(c p) q -> p c q", p=P)
    CPG = GQ // RCH

    block = ctx.enter_context(nc.Block())

    @block.gpsimd
    def _(pool):
        nc.gpsimd.memset(ones[:], 1.0).then_inc(consts, 1)
        nc.gpsimd.memset(ident[:], 0.0).then_inc(consts, 1)
        nc.gpsimd.iota(keyno[:], pattern=[[1, SK]], base=0, channel_multiplier=0,
                       allow_small_or_imprecise_dtypes=True).then_inc(consts, 1)
        nc.gpsimd.iota(rowno[:], pattern=[[0, 1]], base=0, channel_multiplier=1,
                       allow_small_or_imprecise_dtypes=True).then_inc(consts, 1)
        pool.wait_ge(consts, 4)
        nc.gpsimd.affine_select(out=ident[:], in_=ident[:], compare_op=ALU.not_equal, fill=1.0, base=0,
                                pattern=[[-1, P]], channel_multiplier=1).then_inc(consts, 1)

    @block.sync
    def _(sp):
        sp.dma_start(ctx_raw[:], ctxT.rearrange("(e p) k -> p e k", p=P)).then_inc(ctx_in, 16)
        sp.dma_start(w0_raw[:], wkv0.rearrange("(e p) n -> p e n", p=P)).then_inc(w0_in, 16)
        for k in range(CPG):
            sp.dma_start(xr[k][:], x_v[:, :, k * RCH:(k + 1) * RCH]).then_inc(xr_in[k], 16)
        sp.dma_start(nw[:], normw).then_inc(small_in, 16)
        sp.dma_start(bo_sb[:].rearrange("p l c -> p (l c)"), bo).then_inc(small_in, 16)
        for r in range(4):
            sp.dma_start(mrow[r:r + 1, :], masks[r // 2:r // 2 + 1, :]).then_inc(small_in, 16)
            sp.dma_start(tok[r:r + 1, :], tokens).then_inc(small_in, 16)
        for g in range(GROUPS):
            for c in range(CT):
                sp.dma_start(base_dram[g, c * P:(c + 1) * P, :],
                             xT[c * P:(c + 1) * P, g * GQ:(g + 1) * GQ]).then_inc(stored[g], 16)
        sp.dma_start(w_dram, wheads).then_inc(w_copied, 16)
        with sp.Fori(0, GROUPS) as g:
            q_g = query_dram[g].rearrange("(c p) q -> p c q", p=P)
            nxt = (g + 1) % GROUPS
            for k in range(CPG):
                sp.wait_ge(xn_done, g * CPG + (k + 1))
                sp.dma_start(q_g[:, :, k * RCH:(k + 1) * RCH], xr[k][:]).then_inc(xn_out[k], 16)
            for k in range(CPG):
                sp.wait_ge(xn_out[k], g * 16 + 16)
                sp.dma_start(xr[k][:], x_v[:, :, bass.ds(nxt * GQ + k * RCH, RCH)]).then_inc(xr_in[k], 16)
        sp.wait_ge(hi_done, 2 * GROUPS)
        sp.wait_ge(lo_done, 2 * GROUPS)
        for kv in range(2):
            for h in range(HEADS):
                for part, src in enumerate((kv_hi, kv_lo)):
                    r = kv * HD + (h // REP0) * HD0
                    u, s = (h // HH) * GROUPS, h % HH
                    sp.dma_start(
                        kv_dram[u:u + GROUPS, kv, part * HD:part * HD + HD0,
                                s * GK:(s + 1) * GK].rearrange("u p n -> p u n"),
                        src[r:r + HD0, 0, :, :].bitcast(F32)).then_inc(kv_out[kv], 16)
        with sp.Fori(0, LAYERS - 1) as l:
            for m in range(2):
                j = l * 2 + m
                sp.wait_ge(w_hi_done, j + 1)
                sp.wait_ge(w_lo_done, j + 1)
                sp.dma_start(w_raw[:], wkv[(j + 1) % MATS].rearrange("(e p) n -> p e n", p=P)).then_inc(w_in, 16)
                with sp.Fori(0, GROUPS) as g:
                    for half in range(2):
                        tiles = (j * GROUPS + g) * MT + (2 * GROUPS + HMT * (half + 1))
                        sp.wait_ge(hi_done, tiles)
                        sp.wait_ge(lo_done, tiles)
                        u = l * (2 * GROUPS) + g + (2 + half) * GROUPS
                        for part, src in enumerate((kv_hi, kv_lo)):
                            for odd in range(2):
                                sp.dma_start(
                                    kv_dram[u, m, part * HD:(part + 1) * HD, :].rearrange(
                                        "p (t s n) -> p t s n", t=HMT, s=2)[:, :, odd, :],
                                    src[odd * HD:(odd + 1) * HD, half, :, :].bitcast(F32)
                                ).then_inc(kv_out[half], 16)
        for half in range(2):
            sp.wait_ge(kv_out[half], 16 * (2 * HEADS + 4 * MATS * GROUPS))
        for g in range(GROUPS):
            sp.wait_ge(stored[g], 32)
        for k in range(CPG):
            sp.wait_ge(xn_out[k], 16 * GROUPS)
            sp.wait_ge(xr_in[k], 16 * (GROUPS + 1))
        sp.wait_ge(w_copied, 16)
        sp.wait_ge(w_in, 16 * (MATS + 1))

    @block.scalar
    def _(act):
        act.dma_start(w_raw[:], wkv[0].rearrange("(e p) n -> p e n", p=P)).then_inc(w_in, 16)
        act.wait_ge(w0_in, 16)
        nc.scalar.copy(w0_hi[:], w0_raw[:]).then_inc(w0_hi_done, 1)
        act.wait_ge(ctx_in, 16)
        for e in range(ET):
            nc.scalar.copy(ctx_hi[:, e, :], ctx_raw[:, e, :]).then_inc(ctx_hi_done, 1)
        act.wait_ge(w_in, 16)
        for e in range(ET):
            last = nc.scalar.copy(w_hi[0][:, e, :], w_raw[:, e, :])
        last.then_inc(w_hi_done, 1)
        for g in range(GROUPS):
            act.wait_ge(projected, g + 1)
            nc.scalar.copy(kv_hi[:, 0, g, :], ps[:, g, 0:GK]).then_inc(hi_done, 2)
        with act.Fori(0, GROUPS) as g:
            for k in range(CPG):
                act.wait_ge(xr_in[k], g * 16 + 16)
                nc.scalar.activation(xsq[:], xr[k][:], ACT.Square).then_inc(squared, 1)
                act.wait_ge(ms_done, g * CPG + (k + 1))
                nc.scalar.activation(root[:], ms[:], ACT.Sqrt).then_inc(rooted, 1)
        for kv in range(2):
            act.wait_ge(kv_out[kv], 16 * 2 * HEADS)
        with act.Fori(0, LAYERS - 1) as l:
            for m in range(2):
                j = l * 2 + m
                act.wait_ge(w_in, j * 16 + 32)
                for e in range(ET):
                    last = nc.scalar.copy(w_hi[1 - m][:, e, :], w_raw[:, e, :])
                last.then_inc(w_hi_done, 1)
                with act.Fori(0, GROUPS) as g:
                    job = j * GROUPS + g
                    for mt in range(MT):
                        act.wait_ge(projected, job * MT + (GROUPS + mt + 1))
                        if mt % HMT == 0:
                            act.wait_ge(kv_out[mt // HMT], job * 64 + 16 * 2 * HEADS)
                        nc.scalar.copy(kv_hi[:, mt // HMT, mt % HMT, :], ps[:, mt, 0:GK]).then_inc(hi_done, 1)

    @block.vector
    def _(dve):
        steps = [0]

        def then_wait(ins):
            steps[0] += 1
            ins.then_inc(dve_step, 1)
            dve.wait_ge(dve_step, steps[0])

        dve.wait_ge(w0_hi_done, 1)
        nc.vector.tensor_tensor(w0_lo[:], w0_raw[:], w0_hi[:].bitcast(F32), ALU.subtract)
        for e in range(ET):
            dve.wait_ge(ctx_hi_done, e + 1)
            nc.vector.tensor_tensor(ctx_lo[:, e, :], ctx_raw[:, e, :], ctx_hi[:, e, :].bitcast(F32),
                                    ALU.subtract).then_inc(ctx_lo_done, 1)
        dve.wait_ge(w_hi_done, 1)
        nc.vector.tensor_tensor(w_lo[0][:], w_raw[:], w_hi[0][:].bitcast(F32), ALU.subtract).then_inc(w_lo_done, 1)
        dve.wait_ge(hi_done, 2)
        for g in range(GROUPS):
            dve.wait_ge(hi_done, 2 * (g + 1))
            nc.vector.tensor_tensor(kv_lo[:, 0, g, :], ps[:, g, 0:GK], kv_hi[:, 0, g, :].bitcast(F32),
                                    ALU.subtract).then_inc(lo_done, 2)

        dve.wait_ge(small_in, 16 * 10)
        dve.wait_ge(consts, 5)
        then_wait(nc.vector.tensor_scalar(nw2[:], nw[:], SCALE0 / SCALE, None, ALU.mult))
        then_wait(nc.vector.tensor_scalar(sel[:, 0:1], rowno[:], 2.0, None, ALU.is_lt))
        then_wait(nc.vector.tensor_scalar(sel[:, 1:2], rowno[:], 2.0, None, ALU.is_ge))
        then_wait(nc.vector.tensor_scalar(sel[:, 4:5], rowno[:], 0.0, None, ALU.is_equal))
        then_wait(nc.vector.tensor_scalar(sel[:, 2:3], rowno[:], 2.0, sel[:, 4:5], ALU.is_equal, ALU.add))
        then_wait(nc.vector.tensor_scalar(sel[:, 3:4], sel[:, 2:3], -1.0, 1.0, ALU.mult, ALU.add))
        then_wait(nc.vector.tensor_scalar(mrow[:], mrow[:], -1.0, 1.0, ALU.mult, ALU.add))
        then_wait(nc.vector.tensor_scalar(mrow[:], mrow[:], -SUPPRESS, None, ALU.mult))
        then_wait(nc.vector.tensor_copy(mhi[:], mrow[:]))
        then_wait(nc.vector.tensor_tensor(mlo[:], mrow[:], mhi[:].bitcast(F32), ALU.subtract))
        then_wait(nc.vector.tensor_scalar(mlo[:], mlo[:], sel[:, 3:4], None, ALU.mult))
        then_wait(nc.vector.scalar_tensor_tensor(penalty[:], mhi[:].bitcast(F32), sel[:, 2:3], mlo[:],
                                                 ALU.mult, ALU.add))
        then_wait(nc.vector.tensor_copy(tokf[:], tok[:]))
        then_wait(nc.vector.tensor_scalar(wrap[:], tokf[:], 0.0, float(SK), ALU.is_lt, ALU.mult))
        then_wait(nc.vector.tensor_tensor(tokf[:], tokf[:], wrap[:], ALU.add))
        then_wait(nc.vector.memset(key_is[:, 0, :].bitcast(F32), 0.0))
        for l in range(1, LAYERS):
            k = (l - 1) * 4
            then_wait(nc.vector.tensor_scalar(is_a[:], keyno[:], tokf[:, k:k + 1], None, ALU.is_equal))
            then_wait(nc.vector.scalar_tensor_tensor(is_a[:], keyno[:], tokf[:, k + 1:k + 2], is_a[:],
                                                     ALU.is_equal, ALU.max))
            then_wait(nc.vector.tensor_scalar(is_b[:], keyno[:], tokf[:, k + 2:k + 3], None, ALU.is_equal))
            then_wait(nc.vector.scalar_tensor_tensor(is_b[:], keyno[:], tokf[:, k + 3:k + 4], is_b[:],
                                                     ALU.is_equal, ALU.max))
            then_wait(nc.vector.tensor_scalar(other[:], is_b[:], -1.0, 1.0, ALU.mult, ALU.add))
            then_wait(nc.vector.tensor_tensor(is_a[:], is_a[:], other[:], ALU.mult))
            then_wait(nc.vector.tensor_scalar(is_a[:], is_a[:], sel[:, 0:1], None, ALU.mult))
            then_wait(nc.vector.scalar_tensor_tensor(is_b[:], is_b[:], sel[:, 1:2], is_a[:], ALU.mult, ALU.add))
            for s in range(GB):
                then_wait(nc.vector.tensor_copy(key_is[:, l, s * SK:(s + 1) * SK], is_b[:]))

        before = steps[0]
        NS = 4
        with dve.Fori(0, GROUPS) as g:
            for k in range(CPG):
                n = g * CPG + k

                def done(s):
                    return n * NS + (before + s)
                dve.wait_ge(summed, n + 1)
                nc.vector.tensor_scalar(ms[:], ps[:, 4 + k, 0:RCH], 1.0 / C, EPS, ALU.mult, ALU.add).then_inc(ms_done, 1)
                dve.wait_ge(rooted, n + 1)
                nc.vector.reciprocal(inv[:], root[:]).then_inc(dve_step, 1)
                dve.wait_ge(dve_step, done(1))
                nc.vector.scalar_tensor_tensor(corr[:], inv[:], -0.5, inv[:], ALU.mult, ALU.mult).then_inc(dve_step, 1)
                dve.wait_ge(dve_step, done(2))
                nc.vector.tensor_tensor(corr[:], corr[:], ms[:], ALU.mult).then_inc(dve_step, 1)
                dve.wait_ge(dve_step, done(3))
                nc.vector.scalar_tensor_tensor(inv2[:], corr[:], 1.5, inv[:], ALU.add, ALU.mult).then_inc(dve_step, 1)
                dve.wait_ge(dve_step, done(4))
                for c in range(CT):
                    last = nc.vector.scalar_tensor_tensor(xr[k][:, c, :], xr[k][:, c, :], nw2[:, c:c + 1], inv2[:],
                                                          ALU.mult, ALU.mult)
                last.then_inc(xn_done, 1)

        for kv in range(2):
            dve.wait_ge(kv_out[kv], 16 * 2 * HEADS)
        with dve.Fori(0, LAYERS - 1) as l:
            for m in range(2):
                j = l * 2 + m
                dve.wait_ge(w_hi_done, j + 2)
                nc.vector.tensor_tensor(w_lo[1 - m][:], w_raw[:], w_hi[1 - m][:].bitcast(F32),
                                        ALU.subtract).then_inc(w_lo_done, 1)
                with dve.Fori(0, GROUPS) as g:
                    for mt in range(MT):
                        dve.wait_ge(hi_done, (j * GROUPS + g) * MT + (2 * GROUPS + mt + 1))
                        nc.vector.tensor_tensor(kv_lo[:, mt // HMT, mt % HMT, :], ps[:, mt, 0:GK],
                                                kv_hi[:, mt // HMT, mt % HMT, :].bitcast(F32),
                                                ALU.subtract).then_inc(lo_done, 1)

    @block.tensor
    def _(pe):
        def project(out, hi, lo, cols, keys):
            passes = [(a, b) for a, b in ((hi, ctx_hi), (hi, ctx_lo), (lo, ctx_hi))]
            for e in range(ET):
                for n, (a, b) in enumerate(passes):
                    last = nc.tensor.matmul(out, a[:, e, cols], b[:, e, keys], start=(e == 0 and n == 0),
                                            stop=(e == ET - 1 and n == 2))
            return last

        pe.wait_ge(ctx_lo_done, ET)
        for g in range(GROUPS):
            project(ps[:, g, 0:GK], w0_hi, w0_lo, slice(0, P), slice(g * GK, (g + 1) * GK)).then_inc(projected, 1)
        pe.wait_ge(consts, 1)
        with pe.Fori(0, GROUPS) as g:
            for k in range(CPG):
                pe.wait_ge(squared, g * CPG + (k + 1))
                for c in range(CT):
                    last = nc.tensor.matmul(ps[:, 4 + k, 0:RCH], ones[:], xsq[:, c, :], start=(c == 0),
                                            stop=(c == CT - 1))
                last.then_inc(summed, 1)
        pe.wait_ge(ms_done, CPG * GROUPS)
        with pe.Fori(0, LAYERS - 1) as l:
            for m in range(2):
                with pe.Fori(0, GROUPS) as g:
                    pe.wait_ge(w_lo_done, l * 2 + (m + 1))
                    for mt in range(MT):
                        n = ((l * 2 + m) * GROUPS + g) * MT + mt
                        pe.wait_ge(lo_done, n + 1)
                        project(ps[:, mt, 0:GK], w_hi[m], w_lo[m], slice(mt * P, (mt + 1) * P),
                                bass.ds(g * GK, GK)).then_inc(projected, 1)


def attend(nc, ctx, kv_dram, base_dram, query_dram, w_dram, ident, bo_sb, key_is, penalty, stored, outT):
    def sb(name, shape, dt):
        return ctx.enter_context(nc.sbuf_tensor(name, shape, dt))

    def sem(name):
        return ctx.enter_context(nc.semaphore(name))

    wh_hi = [sb(f"wh_hi{m}", [P, HH, C], F32R) for m in range(2)]
    wh_lo = [sb(f"wh_lo{m}", [P, HH, C], F32R) for m in range(2)]
    kv = [sb(f"kv{m}", [P, HH, GK], F32R) for m in range(2)]
    g_hi = sb("g_hi", [P, CT, GB, FLAT], F32R)
    g_lo = sb("g_lo", [P, CT, GB, FLAT], F32R)
    uT = sb("uT", [P, CT, GB, FLAT], F32)
    u_hi = sb("u_hi", [P, GB, FT, C], F32R)
    u_lo = sb("u_lo", [P, GB, FT, C], F32R)
    xq = [sb(f"xq{k}", [P, CT, SQ], F32) for k in range(2)]
    x_hi = [sb(f"x_hi{k}", [P, CT, SQ], F32R) for k in range(2)]
    x_lo = [sb(f"x_lo{k}", [P, CT, SQ], F32R) for k in range(2)]
    probs = [sb(f"probs{k}", [P, FLAT], F32) for k in range(2)]
    pT_hi = sb("pT_hi", [P, FT, SQ], F32R)
    pT_lo = sb("pT_lo", [P, FT, SQ], F32R)
    base = [sb(f"base{k}", [P, CT, SQ], F32) for k in range(2)]
    res = [sb(f"res{k}", [P, CT, SQ], F32) for k in range(2)]
    neg_max = [sb(f"neg_max{k}", [P, HH], F32) for k in range(2)]
    total = [sb(f"total{k}", [P, HH], F32) for k in range(2)]
    recip = [sb(f"recip{k}", [P, HH], F32) for k in range(2)]
    idle = sb("idle", [P, 4], F32)
    scores = ctx.enter_context(nc.psum_tensor("scores", [P, 4, 512], F32))
    work = ctx.enter_context(nc.psum_tensor("work", [P, 4, 512], F32))

    kv_in = [sem(f"kv_in{m}") for m in range(2)]
    wh_in = sem("wh_in")
    xq_in = [sem(f"xq_in{k}") for k in range(2)]
    base_in = [sem(f"base_in{k}") for k in range(2)]
    wh_hi_done = sem("wh_hi_done")
    wh_lo_done = sem("wh_lo_done")
    x_hi_done = sem("x_hi_done")
    x_split = sem("x_split")
    staged = sem("staged")
    stage_hi = sem("stage_hi")
    g_lo_done = sem("g_lo_done")
    u_lo_done = sem("u_lo_done")
    scored = sem("scored")
    maxed = sem("maxed")
    exped = sem("exped")
    summed = sem("total_done")
    recips = sem("recips")
    normed = sem("normed")
    turned = sem("turned")
    pT_hi_done = sem("pT_hi_done")
    pT_lo_done = sem("pT_lo_done")
    attended = sem("attended")
    res_done = sem("res_done")
    zeroed = sem("zeroed")

    block = ctx.enter_context(nc.Block())
    LATE = UNITS - GROUPS
    LAST_UNIT = UNITS - 1

    @block.sync
    def _(sp):
        def load_kv(v, m, rows):
            for part in range(2):
                sp.dma_start(kv[m][part * HD:part * HD + rows, :, :].bitcast(F32),
                             kv_dram[v, m, part * HD:part * HD + rows, :].rearrange(
                                 "p (h n) -> p h n", h=HH)).then_inc(kv_in[m], 16)

        def load_weights(lh):
            for m in range(2):
                for part in range(2):
                    sp.dma_start(wh_lo[m][part * HD:(part + 1) * HD, :, :].bitcast(F32),
                                 w_dram[lh, m].rearrange("p (h n) -> p h n", h=HH)).then_inc(wh_in, 16)

        def cols(b):
            return slice(b * SQ, (b + 1) * SQ)

        def load_queries(v, b):
            src = (v // (2 * GROUPS)) * (2 * GROUPS) + v % GROUPS
            sp.dma_start(xq[b % 2][:], query_dram[src].rearrange("(c p) q -> p c q", p=P)[:, :, cols(b)]
                         ).then_inc(xq_in[b % 2], 16)

        def load_base(v, b):
            sp.dma_start(base[b % 2][:], base_dram[v].rearrange("(c p) q -> p c q", p=P)[:, :, cols(b)]
                         ).then_inc(base_in[b % 2], 16)

        def store(u, b, late):
            sp.wait_ge(res_done, u * GB + (b + 3))
            if late is None:
                for dst in (base_dram, query_dram):
                    sp.dma_start(dst[u + GROUPS].rearrange("(c p) q -> p c q", p=P)[:, :, cols(b)],
                                 res[b % 2][:]).then_inc(stored[b], 16)
            else:
                for c in range(CT):
                    sp.dma_start(outT[c * P:(c + 1) * P, bass.ds(late * GQ + b * SQ, SQ)],
                                 res[b % 2][:, c, :]).then_inc(stored[b], 16)

        def unit(u, next_rows, weights=None, late=None):
            if next_rows:
                sp.wait_ge(staged, u * STAGE + N_G)
                load_kv(u + 1, 0, next_rows)
                sp.wait_ge(staged, u * STAGE + 2 * N_G)
                load_kv(u + 1, 1, next_rows)
            for b in range(2):
                sp.wait_ge(res_done, u * GB + (b + 1))
                sp.wait_ge(stored[b], u * 32 + 32)
                load_base(u, b)
            for b in range(2, GB):
                sp.wait_ge(stored[b], u * 32 + 32)
                sp.wait_ge(x_split, u * GB + (b - 1))
                load_queries(u, b)
            if weights is not None:
                sp.wait_ge(staged, u * STAGE + STAGE)
                load_weights(weights)
            for b in range(2):
                store(u, b, late)
                load_base(u, b + 2)
                if next_rows:
                    sp.wait_ge(stored[b], u * 32 + 64)
                    sp.wait_ge(x_split, u * GB + (b + 3))
                    load_queries(u + 1, b)
            for b in range(2, GB):
                store(u, b, late)

        sp.wait_ge(zeroed, 2)
        load_kv(0, 0, HD0)
        load_kv(0, 1, HD0)
        load_weights(0)
        load_queries(0, 0)
        load_queries(0, 1)
        G3 = GROUPS - 1
        for lh in range(2):
            with sp.Fori(lh * GROUPS, lh * GROUPS + G3) as u:
                unit(u, HD0)
            unit(lh * GROUPS + G3, HD0 if lh == 0 else HD, weights=lh + 1)
        with sp.Fori(2, HALVES - 1) as lh:
            with sp.Fori(0, G3) as g:
                unit(lh * GROUPS + g, HD)
            unit(lh * GROUPS + G3, HD, weights=lh + 1)
        with sp.Fori(0, G3) as g:
            unit(g + LATE, HD, late=g)
        unit(UNITS - 1, 0, late=G3)
        for b in range(GB):
            sp.wait_ge(stored[b], (UNITS + 1) * 32)

    def in_turn(eng, unit):
        with eng.Fori(0, HALVES - 1) as lh:
            with eng.Fori(0, GROUPS - 1) as g:
                unit(lh * GROUPS + g, lh, False)
            unit(lh * GROUPS + (GROUPS - 1), lh, True)
        with eng.Fori(0, GROUPS - 1) as g:
            unit(g + LATE, HALVES - 1, False)
        unit(LAST_UNIT, HALVES - 1, False)

    @block.scalar
    def _(act):
        def weights_hi(lh):
            act.wait_ge(wh_in, lh * 64 + 64)
            for m in range(2):
                nc.scalar.copy(wh_hi[m][:], wh_lo[m][:].bitcast(F32)).then_inc(wh_hi_done, 1)

        def exponents(u, i):
            act.wait_ge(maxed, u * ITEMS + (i + 1))
            act.wait_ge(turned, u * ITEMS + (i + 1))
            k = i % 2
            for h in range(HH):
                last = nc.scalar.activation(
                    probs[k][:, h * SK:(h + 1) * SK],
                    scores[:, 2 * k + h // 4, (h % 4) * SK:(h % 4 + 1) * SK],
                    ACT.Exp, bias=neg_max[k][:, h:h + 1])
            last.then_inc(exped, 1)

        def unit(u, lh, weights):
            for j in range(2 * N_G):
                h, c = j % N_G // CT, j % CT
                dst = (g_hi if j < N_G else uT)[:, c, :, h * SK:(h + 1) * SK]
                act.wait_ge(staged, u * STAGE + (j + 1))
                nc.scalar.copy(dst, work[:, j % 4, 0:GK].rearrange("p (b k) -> p b k", b=GB)).then_inc(stage_hi, 1)
                if j == N_G + 4:
                    exponents(u, 0)
                if j == N_G + 9:
                    exponents(u, 1)
            for s in range(N_U):
                b, t = s // FT, s % FT
                act.wait_ge(staged, u * STAGE + (2 * N_G + s + 1))
                nc.scalar.copy(u_hi[0:rows_of(t), b, t, :], work[0:rows_of(t), s % 4, 0:C]).then_inc(stage_hi, 1)
            for i in range(ITEMS):
                if i + 2 < ITEMS:
                    exponents(u, i + 2)
                act.wait_ge(turned, u * ITEMS + (i + 3))
                q = slice(i % QT * P, (i % QT + 1) * P)
                nc.scalar.copy(pT_hi[:, 0:FT - 1, q], work[:, 0, :].rearrange("p (t q) -> p t q", q=P))
                nc.scalar.copy(pT_hi[0:LAST, FT - 1, q], work[0:LAST, 1, 0:P]).then_inc(pT_hi_done, 1)
                if weights and i == ITEMS - 2:
                    weights_hi(lh + 1)

        act.wait_ge(zeroed, 3)
        nc.scalar.activation(idle[:, 3:4], idle[:, 2:3], ACT.Exp).then_inc(exped, 2)
        weights_hi(0)
        in_turn(act, unit)

    @block.vector
    def _(dve):
        def weights_lo(lh):
            for m in range(2):
                dve.wait_ge(wh_hi_done, lh * 2 + (m + 1))
                nc.vector.tensor_tensor(wh_lo[m][:], wh_lo[m][:].bitcast(F32), wh_hi[m][:].bitcast(F32),
                                        ALU.subtract).then_inc(wh_lo_done, 1)

        def split_queries(v, b, first=False):
            k = b % 2
            dve.wait_ge(xq_in[k], v * 32 + 16 * (b // 2 + 1))
            if not first:
                dve.wait_ge(scored, v * ITEMS + 2 * (b - 1))
            nc.vector.tensor_scalar(x_hi[k][:], xq[k][:], SCALE, None, ALU.mult).then_inc(x_hi_done, 1)
            dve.wait_ge(x_hi_done, v * GB + (b + 1))
            nc.vector.scalar_tensor_tensor(x_lo[k][:], xq[k][:], SCALE, x_hi[k][:].bitcast(F32),
                                           ALU.mult, ALU.subtract).then_inc(x_split, 1)

        def maxima(u, i):
            k = i % 2
            dve.wait_ge(scored, u * ITEMS + (i + 1))
            nc.vector.tensor_reduce(neg_max[k][:].rearrange("p (a h) -> p a h", a=2),
                                    scores[:, 2 * k:2 * k + 2, 0:HFLAT].rearrange("p a (h n) -> p a h n", n=SK),
                                    AX.X, ALU.max, negate=True).then_inc(maxed, 1)

        def totals(u, i):
            k = i % 2
            dve.wait_ge(exped, u * ITEMS + (i + 3))
            nc.vector.tensor_reduce(total[k][:], probs[k][:].rearrange("p (h n) -> p h n", n=SK),
                                    AX.X, ALU.add).then_inc(summed, 1)
            dve.wait_ge(summed, u * ITEMS + (i + 1))
            nc.vector.reciprocal(recip[k][:], total[k][:]).then_inc(recips, 1)

        def result(u, lh, b):
            k = b % 2
            dve.wait_ge(attended, u * GB + (b + 1))
            dve.wait_ge(base_in[k], u * 32 + 16 * (b // 2 + 1))
            dve.wait_ge(stored[(b + 2) % GB], u * 32 + 32 * (1 + b // 2))
            for c in range(CT):
                last = nc.vector.scalar_tensor_tensor(
                    res[k][:, c, :], work[:, 2 + k, c * SQ:(c + 1) * SQ], bo_sb[:, lh, c:c + 1],
                    base[k][:, c, :], ALU.add, ALU.add)
            last.then_inc(res_done, 1)

        def unit(u, lh, weights):
            for j in range(N_G):
                h, c = j // CT, j % CT
                at = (slice(None), c, slice(None), slice(h * SK, (h + 1) * SK))
                dve.wait_ge(stage_hi, u * STAGE + (j + 1))
                nc.vector.tensor_tensor(g_lo[at], work[:, j % 4, 0:GK].rearrange("p (b k) -> p b k", b=GB),
                                        g_hi[at].bitcast(F32), ALU.subtract).then_inc(g_lo_done, 1)
            for i in range(2):
                maxima(u, i)
            for i in range(2):
                totals(u, i)
            for s in range(N_U):
                b, t = s // FT, s % FT
                dve.wait_ge(stage_hi, u * STAGE + (2 * N_G + s + 1))
                nc.vector.tensor_tensor(u_lo[0:rows_of(t), b, t, :], work[0:rows_of(t), s % 4, 0:C],
                                        u_hi[0:rows_of(t), b, t, :].bitcast(F32),
                                        ALU.subtract).then_inc(u_lo_done, 1)
            for i in range(ITEMS):
                if i + 2 < ITEMS:
                    maxima(u, i + 2)
                dve.wait_ge(pT_hi_done, u * ITEMS + (i + 1))
                q = slice(i % QT * P, (i % QT + 1) * P)
                nc.vector.tensor_tensor(pT_lo[:, 0:FT - 1, q], work[:, 0, :].rearrange("p (t q) -> p t q", q=P),
                                        pT_hi[:, 0:FT - 1, q].bitcast(F32), ALU.subtract)
                nc.vector.tensor_tensor(pT_lo[0:LAST, FT - 1, q], work[0:LAST, 1, 0:P],
                                        pT_hi[0:LAST, FT - 1, q].bitcast(F32), ALU.subtract).then_inc(pT_lo_done, 1)
                if i + 2 < ITEMS:
                    totals(u, i + 2)
                if i in (1, 2):
                    split_queries(u, i + 1)
                if i in (4, 6) and u is not LAST_UNIT:
                    split_queries(u + 1, i // 2 - 2)
                if i in (2, 4, 6):
                    result(u, lh, i // 2 - 1)
            if weights:
                weights_lo(lh + 1)
            result(u, lh, GB - 1)

        for m in range(2):
            nc.vector.memset(kv[m][:].bitcast(F32), 0.0).then_inc(zeroed, 1)
        nc.vector.memset(idle[:, 0:1], 0.0).then_inc(pT_lo_done, 1)
        nc.vector.memset(idle[:, 1:2], 0.0).then_inc(res_done, 2)
        nc.vector.memset(idle[:, 2:3], 0.0).then_inc(zeroed, 1)
        weights_lo(0)
        split_queries(0, 0, first=True)
        split_queries(0, 1, first=True)
        in_turn(dve, unit)

    @block.gpsimd
    def _(pool):
        with pool.Fori(0, UNITS) as u:
            for i in range(ITEMS):
                k = i % 2
                pool.wait_ge(recips, u * ITEMS + (i + 1))
                p3 = probs[k][:].rearrange("p (h n) -> p h n", n=SK)
                nc.gpsimd.tensor_tensor(p3, p3, recip[k][:].unsqueeze(2).to_broadcast((P, HH, SK)),
                                        ALU.mult).then_inc(normed, 1)

    @block.tensor
    def _(pe):
        def product(u, j):
            m, h, c = j // N_G, j % N_G // CT, j % CT
            if j == 0:
                pe.wait_ge(kv_in[0], u * 32 + 32)
                pe.wait_ge(pT_lo_done, u * ITEMS + 1)
                pe.wait_ge(res_done, u * GB + 2)
            if j == N_G:
                pe.wait_ge(kv_in[1], u * 32 + 32)
            if j >= 4:
                pe.wait_ge(stage_hi, u * STAGE + (j - 3))
                if j - 4 < N_G:
                    pe.wait_ge(g_lo_done, u * N_G + (j - 3))
            for n, w in enumerate((wh_hi, wh_lo)):
                last = nc.tensor.matmul(work[:, j % 4, 0:GK], w[m][:, h, c * P:(c + 1) * P], kv[m][:, h, :],
                                        start=(n == 0), stop=(n == 1))
            last.then_inc(staged, 1)

        def turn_u(u, s):
            b, t = s // FT, s % FT
            pe.wait_ge(stage_hi, u * STAGE + (2 * N_G if s < 4 else 2 * N_G + s - 3))
            if s >= 4:
                pe.wait_ge(u_lo_done, u * N_U + (s - 3))
            n = rows_of(t)
            for c in range(CT):
                last = nc.tensor.transpose(work[0:n, s % 4, c * P:(c + 1) * P], uT[:, c, b, t * P:t * P + n], ident[:])
            last.then_inc(staged, 1)

        def score(u, lh, i):
            b, q, k = i // QT, slice(i % QT * P, (i % QT + 1) * P), i % 2
            if i == 0:
                pe.wait_ge(stage_hi, u * STAGE + N_G)
                pe.wait_ge(g_lo_done, u * N_G + N_G)
            pe.wait_ge(x_split, u * GB + (b + 1))
            pe.wait_ge(exped, u * ITEMS + (i + 1))
            x = (x_hi[b % 2], x_lo[b % 2])
            out = [scores[:, 2 * k + a, 0:HFLAT] for a in range(2)]
            for c in range(CT):
                for n, (xp, gp) in enumerate(((x[0], g_hi), (x[0], g_lo), (x[1], g_hi))):
                    for a in range(2):
                        nc.tensor.matmul(out[a], xp[:, c, q], gp[:, c, b, a * HFLAT:(a + 1) * HFLAT],
                                                start=(c == 0 and n == 0), stop=False)
            for a in range(2):
                last = nc.tensor.matmul(out[a], penalty[:, q], key_is[:, lh // 2, :], start=False, stop=True)
            last.then_inc(scored, 1)

        def turn(u, i):
            if i == 0:
                pe.wait_ge(u_lo_done, u * N_U + N_U)
            pe.wait_ge(normed, u * ITEMS + (i + 1))
            pe.wait_ge(pT_lo_done, u * ITEMS + (i + 1))
            for t in range(FT):
                n = rows_of(t)
                out = work[:, 0, t * P:(t + 1) * P] if t < FT - 1 else work[0:n, 1, 0:P]
                last = nc.tensor.transpose(out, probs[i % 2][:, t * P:t * P + n], ident[:])
            last.then_inc(turned, 1)

        def attend_values(u, b):
            pe.wait_ge(pT_lo_done, u * ITEMS + (2 * b + 3))
            pe.wait_ge(res_done, u * GB + (b + 1))
            for c in range(CT):
                for t in range(FT):
                    r = rows_of(t)
                    for n, (up, pp) in enumerate(((u_hi, pT_hi), (u_hi, pT_lo), (u_lo, pT_hi))):
                        last = nc.tensor.matmul(work[:, 2 + b % 2, c * SQ:(c + 1) * SQ],
                                                up[0:r, b, t, c * P:(c + 1) * P], pp[0:r, t, :],
                                                start=(t == 0 and n == 0), stop=(t == FT - 1 and n == 2))
            last.then_inc(attended, 1)

        def unit(u, lh):
            for j in range(N_G):
                product(u, j)
            score(u, lh, 0)
            score(u, lh, 1)
            for j in range(N_G, 2 * N_G):
                product(u, j)
            for s in range(N_U):
                turn_u(u, s)
            for i in range(ITEMS):
                if i + 2 < ITEMS:
                    score(u, lh, i + 2)
                if i in (2, 4, 6):
                    attend_values(u, i // 2 - 1)
                turn(u, i)
            attend_values(u, GB - 1)

        nc.tensor.transpose(work[:, 0, 0:P], ident[:], ident[:]).then_inc(turned, 2)
        with pe.Fori(0, HALVES) as lh:
            with pe.Fori(0, GROUPS) as g:
                pe.wait_ge(wh_lo_done, lh * 2 + 2)
                unit(lh * GROUPS + g, lh)


def kernel(**inputs):
    import numpy as np
    import concourse.bacc as bacc
    from concourse.bass_utils import run_bass_kernel_spmd

    a = {k: np.asarray(v) for k, v in inputs.items()}
    L = [f"L{l}_xattn_" for l in range(LAYERS)]

    def heads_first(w, d):
        out = np.zeros((2, HD, HH, C), np.float32)
        out[:, :d] = w.reshape(2, HH, d, C).transpose(0, 2, 1, 3)
        return out.reshape(2, HD, HH * C)

    wheads = np.zeros((HALVES, 2, HD, HH * C), np.float32)
    bo = np.zeros((P, HALVES, CT), np.float32)
    for l in range(LAYERS):
        q, o, d = ("wq", "wo", HD0) if l == 0 else ("Wq", "Wo", HD)
        wheads[2 * l:2 * l + 2, 0] = heads_first(a[L[l] + q].T, d)
        wheads[2 * l:2 * l + 2, 1] = heads_first(a[L[l] + o], d)
        if l:
            bo[:, 2 * l, :] = a[L[l] + "bo"].reshape(CT, P).T
    arrays = {
        "xT": a["x"].reshape(B * SQ, C).T,
        "ctxT": a["ctx_2048"].reshape(B * SK, E).T,
        "wkv0": np.concatenate([a[L[0] + "wk"], a[L[0] + "wv"]], axis=1),
        "wkv": np.stack([a[L[l] + w] for l in range(1, LAYERS) for w in ("Wk", "Wv")]),
        "wheads": wheads,
        "normw": a[L[0] + "norm_w"].reshape(CT, P).T,
        "bo": bo.reshape(P, HALVES * CT),
        "masks": np.stack([a["mask_S_fk1"], a["mask_S_fk0"]]),
        "tokens": np.concatenate([a[L[l] + f"token_indices_{s}"] for l in range(1, LAYERS) for s in "AB"])[None, :],
    }
    arrays = {k: np.ascontiguousarray(v) for k, v in arrays.items()}
    nc = bacc.Bacc("TRN2", target_bir_lowering=False, num_devices=1)
    aps = {k: nc.dram_tensor(k, v.shape, mybir.dt.from_np(v.dtype), kind="ExternalInput").ap()
           for k, v in arrays.items()}
    outT = nc.dram_tensor("outT", (C, B * SQ), F32, kind="ExternalOutput").ap()
    build(nc, outT=outT, **aps)
    r = run_bass_kernel_spmd(nc, [arrays], core_ids=[0])
    return np.ascontiguousarray(r.results[0]["outT"].T).reshape(B, SQ, C)
```

```python
from contextlib import ExitStack

import concourse.bass as bass
from concourse import mybir

F32 = mybir.dt.float32
F32R = mybir.dt.float32r
I32 = mybir.dt.int32
ALU = mybir.AluOpType
ACT = mybir.ActivationFunctionType
AX = mybir.AxisListType

P = 128
LAYERS = 4
B, SQ, C = 16, 256, 256
SK, E = 77, 512
HEADS, HD = 16, 64
HD0, KVH0 = 16, 4
REP0 = HEADS // KVH0
CT, ET, QT = C // P, E // P, SQ // P
GB = 4
GROUPS = B // GB
GK, GQ = GB * SK, GB * SQ
HH = HEADS // 2
FLAT = HH * SK
HFLAT = FLAT // 2
FT = (FLAT + P - 1) // P
LAST = FLAT - (FT - 1) * P
HALVES = LAYERS * 2
UNITS = HALVES * GROUPS
ITEMS = GB * QT
MT = HEADS * HD // P
HMT = MT // 2
MATS = 2 * (LAYERS - 1)
N_G = HH * CT
N_U = GB * FT // 2
RCH = 512
EPS = 1e-5
SUPPRESS = 20.0
SCALE = HD ** -0.5
SCALE0 = HD0 ** -0.5
KV0_DMAS = KVH0 * 2 * REP0


def rows_of(t):
    return LAST if t == FT - 1 else P


def build(nc, xT, ctxT, wkv0, wkv, wheads, normw, bo, masks, tokens, outT):
    kv_dram = nc.dram_tensor("kv_dram", (UNITS, 2, P, HH * GK), F32, kind="Internal").ap()
    base_dram = nc.dram_tensor("base_dram", (UNITS, C, GQ), F32, kind="Internal").ap()
    query_dram = nc.dram_tensor("query_dram", (UNITS, C, GQ), F32, kind="Internal").ap()
    w_dram = nc.dram_tensor("w_dram", (HALVES, 2, HD, HH * C), F32, kind="Internal").ap()

    with ExitStack() as whole:
        def sb(name, shape, dt):
            return whole.enter_context(nc.sbuf_tensor(name, shape, dt))

        def sem(name):
            return whole.enter_context(nc.semaphore(name))

        ident = sb("ident", [P, P], F32)
        bo_sb = sb("bo_sb", [P, HALVES, CT], F32)
        key_is = sb("key_is", [4, LAYERS, GK], F32R)
        penalty = sb("penalty", [4, SQ], F32R)
        stored = [sem(f"stored{b}") for b in range(GB)]
        with ExitStack() as part:
            prepare(nc, part, xT, ctxT, wkv0, wkv, wheads, normw, bo, masks, tokens,
                    kv_dram, base_dram, query_dram, w_dram, ident, bo_sb, key_is, penalty, stored)
        with ExitStack() as part:
            attend(nc, part, kv_dram, base_dram, query_dram, w_dram,
                   ident, bo_sb, key_is, penalty, stored, outT)


def prepare(nc, ctx, xT, ctxT, wkv0, wkv, wheads, normw, bo, masks, tokens,
            kv_dram, base_dram, query_dram, w_dram, ident, bo_sb, key_is, penalty, stored):
    def sb(name, shape, dt):
        return ctx.enter_context(nc.sbuf_tensor(name, shape, dt))

    def sem(name):
        return ctx.enter_context(nc.semaphore(name))

    ctx_raw = sb("ctx_raw", [P, ET, B * SK], F32)
    ctx_hi = sb("ctx_hi", [P, ET, B * SK], F32R)
    ctx_lo = sb("ctx_lo", [P, ET, B * SK], F32R)
    w0_raw = sb("w0_raw", [P, ET, P], F32)
    w0_hi = sb("w0_hi", [P, ET, P], F32R)
    w0_lo = sb("w0_lo", [P, ET, P], F32R)
    w_raw = sb("w_raw", [P, ET, MT * P], F32)
    w_hi = [sb(f"w_hi{m}", [P, ET, MT * P], F32R) for m in range(2)]
    w_lo = [sb(f"w_lo{m}", [P, ET, MT * P], F32R) for m in range(2)]
    kv_hi = sb("kv_hi", [P, 2, HMT, GK], F32R)
    kv_lo = sb("kv_lo", [P, 2, HMT, GK], F32R)
    xr = sb("xr", [P, CT, RCH], F32)
    xsq = sb("xsq", [P, CT, RCH], F32)
    ms = sb("ms", [P, RCH], F32)
    root = sb("root", [P, RCH], F32)
    inv = sb("inv", [P, RCH], F32)
    corr = sb("corr", [P, RCH], F32)
    inv2 = sb("inv2", [P, RCH], F32)
    ones = sb("ones", [P, P], F32)
    kv_scale = sb("kv_scale", [P, 1], F32)
    nw = sb("nw", [P, CT], F32)
    nw2 = sb("nw2", [P, CT], F32)
    tok = sb("tok", [4, (LAYERS - 1) * 4], I32)
    tokf = sb("tokf", [4, (LAYERS - 1) * 4], F32)
    wrap = sb("wrap", [4, (LAYERS - 1) * 4], F32)
    keyno = sb("keyno", [4, SK], F32)
    rowno = sb("rowno", [4, 1], F32)
    sel = sb("sel", [4, 8], F32)
    is_a = sb("is_a", [4, SK], F32)
    is_b = sb("is_b", [4, SK], F32)
    other = sb("other", [4, SK], F32)
    mrow = sb("mrow", [4, SQ], F32)
    mhi = sb("mhi", [4, SQ], F32R)
    mlo = sb("mlo", [4, SQ], F32)
    ps = ctx.enter_context(nc.psum_tensor("proj_ps", [P, 8, 512], F32))

    small_in = sem("small_in")
    ctx_in = sem("ctx_in")
    w0_in = sem("w0_in")
    w_in = sem("w_in")
    w_copied = sem("w_copied")
    xr_in = sem("xr_in")
    xn_out = sem("xn_out")
    kv_out = [sem(f"kv_out{h}") for h in range(2)]
    consts = sem("consts")
    ctx_hi_done = sem("ctx_hi_done")
    ctx_lo_done = sem("ctx_lo_done")
    w0_hi_done = sem("w0_hi_done")
    w_hi_done = sem("w_hi_done")
    w_lo_done = sem("w_lo_done")
    squared = sem("squared")
    summed = sem("summed")
    ms_done = sem("ms_done")
    rooted = sem("rooted")
    xn_done = sem("xn_done")
    projected = sem("projected")
    kv_scaled = sem("kv_scaled")
    hi_done = sem("hi_done")
    lo_done = sem("lo_done")
    dve_step = sem("dve_step")

    x_v = xT.rearrange("(c p) q -> p c q", p=P)
    CPG = GQ // RCH

    block = ctx.enter_context(nc.Block())

    @block.gpsimd
    def _(pool):
        nc.gpsimd.memset(ones[:], 1.0).then_inc(consts, 1)
        nc.gpsimd.memset(ident[:], 0.0).then_inc(consts, 1)
        nc.gpsimd.iota(keyno[:], pattern=[[1, SK]], base=0, channel_multiplier=0,
                       allow_small_or_imprecise_dtypes=True).then_inc(consts, 1)
        nc.gpsimd.iota(rowno[:], pattern=[[0, 1]], base=0, channel_multiplier=1,
                       allow_small_or_imprecise_dtypes=True).then_inc(consts, 1)
        pool.wait_ge(consts, 4)
        nc.gpsimd.affine_select(out=ident[:], in_=ident[:], compare_op=ALU.not_equal, fill=1.0, base=0,
                                pattern=[[-1, P]], channel_multiplier=1).then_inc(consts, 1)

    @block.sync
    def _(sp):
        sp.dma_start(ctx_raw[:], ctxT.rearrange("(e p) k -> p e k", p=P)).then_inc(ctx_in, 16)
        sp.dma_start(w0_raw[:], wkv0.rearrange("(e p) n -> p e n", p=P)).then_inc(w0_in, 16)
        sp.dma_start(xr[:], x_v[:, :, 0:RCH]).then_inc(xr_in, 16)
        sp.dma_start(nw[:], normw).then_inc(small_in, 16)
        sp.dma_start(bo_sb[:].rearrange("p l c -> p (l c)"), bo).then_inc(small_in, 16)
        for r in range(4):
            sp.dma_start(mrow[r:r + 1, :], masks[r // 2:r // 2 + 1, :]).then_inc(small_in, 16)
            sp.dma_start(tok[r:r + 1, :], tokens).then_inc(small_in, 16)
        for g in range(GROUPS):
            for c in range(CT):
                sp.dma_start(base_dram[g, c * P:(c + 1) * P, :],
                             xT[c * P:(c + 1) * P, g * GQ:(g + 1) * GQ]).then_inc(stored[g], 16)
        sp.dma_start(w_dram, wheads).then_inc(w_copied, 16)
        sp.wait_ge(lo_done, GROUPS)
        for kv in range(2):
            for h in range(HEADS):
                for part, src in enumerate((kv_hi, kv_lo)):
                    r = kv * HD + (h // REP0) * HD0
                    u, s = (h // HH) * GROUPS, h % HH
                    sp.dma_start(
                        kv_dram[u:u + GROUPS, kv, part * HD:part * HD + HD0,
                                s * GK:(s + 1) * GK].rearrange("u p n -> p u n"),
                        src[r:r + HD0, 0, :, :].bitcast(F32)).then_inc(kv_out[kv], 16)

        def matrix(j, m, chunks):
            following = sp.snap((j + 1) % MATS)
            sp.wait_ge(w_lo_done, j + 1)
            sp.dma_start(w_raw[:], wkv[following].rearrange("(e p) n -> p e n", p=P)).then_inc(w_in, 16)
            with sp.Fori(0, GROUPS) as g:
                for half in range(2):
                    sp.wait_ge(lo_done, (j * GROUPS + g) * MT + (GROUPS + HMT * (half + 1)))
                    u = (j - m) * GROUPS + g + (2 + half) * GROUPS
                    for part, src in enumerate((kv_hi, kv_lo)):
                        for odd in range(2):
                            sp.dma_start(
                                kv_dram[u, m, part * HD:(part + 1) * HD, :].rearrange(
                                    "p (t s n) -> p t s n", t=HMT, s=2)[:, :, odd, :],
                                src[odd * HD:(odd + 1) * HD, half, :, :].bitcast(F32)
                            ).then_inc(kv_out[half], 16)
                if chunks:
                    n = m * GROUPS + g
                    nxt = sp.snap((n + 1) % (GROUPS * CPG))
                    group, place = sp.snap(n // CPG), sp.snap(n % CPG)
                    sp.wait_ge(xn_done, n + 1)
                    sp.dma_start(query_dram[group].rearrange("(c p) q -> p c q", p=P)[
                        :, :, bass.ds(place * RCH, RCH)], xr[:]).then_inc(xn_out, 16)
                    sp.wait_ge(xn_out, n * 16 + 16)
                    sp.dma_start(xr[:], x_v[:, :, bass.ds(nxt * RCH, RCH)]).then_inc(xr_in, 16)

        for m in range(2):
            matrix(m, m, True)
        with sp.Fori(1, LAYERS - 1) as l:
            for m in range(2):
                matrix(l * 2 + m, m, False)
        for half in range(2):
            sp.wait_ge(kv_out[half], 16 * (2 * HEADS + 4 * MATS * GROUPS))
        for g in range(GROUPS):
            sp.wait_ge(stored[g], 32)
        sp.wait_ge(xn_out, 16 * GROUPS * CPG)
        sp.wait_ge(xr_in, 16 * (GROUPS * CPG + 1))
        sp.wait_ge(w_copied, 16)
        sp.wait_ge(w_in, 16 * (MATS + 1))

    def matrices(eng, split, job):
        def matrix(j, m, chunks):
            for late in range(2):
                with eng.Fori(late * 2, late * 2 + 2) as g:
                    job(j, m, g, chunks)
                if not late:
                    split(j + 1, 1 - m)
        for m in range(2):
            matrix(m, m, True)
        with eng.Fori(1, LAYERS - 1) as l:
            for m in range(2):
                matrix(l * 2 + m, m, False)

    @block.scalar
    def _(act):
        def split(j, m):
            act.wait_ge(w_in, j * 16 + 16)
            for e in range(ET):
                last = nc.scalar.copy(w_hi[m][:, e, :], w_raw[:, e, :])
            last.then_inc(w_hi_done, 1)

        def job(j, m, g, chunks):
            n = j * GROUPS + g
            for mt in range(MT):
                if chunks and mt == 0:
                    act.wait_ge(xr_in, n * 16 + 16)
                    nc.scalar.activation(xsq[:], xr[:], ACT.Square).then_inc(squared, 1)
                if chunks and mt == 2:
                    act.wait_ge(ms_done, n + 1)
                    nc.scalar.activation(root[:], ms[:], ACT.Sqrt).then_inc(rooted, 1)
                act.wait_ge(projected, n * MT + (GROUPS + mt + 1))
                if mt % HMT == 0:
                    act.wait_ge(kv_out[mt // HMT], n * 64 + 16 * 2 * HEADS)
                dst, src = kv_hi[:, mt // HMT, mt % HMT, :], ps[:, mt % 4, 0:GK]
                if m == 0:
                    ins = nc.scalar.mul(dst, src, SCALE)
                else:
                    ins = nc.scalar.copy(dst, src)
                ins.then_inc(hi_done, 1)

        act.dma_start(w_raw[:], wkv[0].rearrange("(e p) n -> p e n", p=P)).then_inc(w_in, 16)
        act.wait_ge(w0_in, 16)
        nc.scalar.copy(w0_hi[:], w0_raw[:]).then_inc(w0_hi_done, 1)
        act.wait_ge(ctx_in, 16)
        for e in range(ET):
            nc.scalar.copy(ctx_hi[:, e, :], ctx_raw[:, e, :]).then_inc(ctx_hi_done, 1)
        split(0, 0)
        act.wait_ge(kv_scaled, 1)
        for g in range(GROUPS):
            act.wait_ge(projected, g + 1)
            nc.scalar.mul(kv_hi[:, 0, g, :], ps[:, g, 0:GK], kv_scale[:]).then_inc(hi_done, 1)
        for kv in range(2):
            act.wait_ge(kv_out[kv], 16 * 2 * HEADS)
        matrices(act, split, job)

    @block.vector
    def _(dve):
        steps = [0]

        def then_wait(ins):
            steps[0] += 1
            ins.then_inc(dve_step, 1)
            dve.wait_ge(dve_step, steps[0])

        def split(j, m):
            dve.wait_ge(w_hi_done, j + 1)
            nc.vector.tensor_tensor(w_lo[m][:], w_raw[:], w_hi[m][:].bitcast(F32),
                                    ALU.subtract).then_inc(w_lo_done, 1)

        def tile_lo(n, mt, m):
            dve.wait_ge(hi_done, n * MT + (GROUPS + mt + 1))
            dst, src = kv_lo[:, mt // HMT, mt % HMT, :], ps[:, mt % 4, 0:GK]
            hi = kv_hi[:, mt // HMT, mt % HMT, :].bitcast(F32)
            if m == 0:
                ins = nc.vector.scalar_tensor_tensor(dst, src, SCALE, hi, ALU.mult, ALU.subtract)
            else:
                ins = nc.vector.tensor_tensor(dst, src, hi, ALU.subtract)
            ins.then_inc(lo_done, 1)

        nc.vector.memset(kv_scale[0:HD, :], SCALE).then_inc(kv_scaled, 1)
        nc.vector.memset(kv_scale[HD:P, :], 1.0).then_inc(kv_scaled, 1)
        dve.wait_ge(w0_hi_done, 1)
        nc.vector.tensor_tensor(w0_lo[:], w0_raw[:], w0_hi[:].bitcast(F32), ALU.subtract)
        for e in range(ET):
            dve.wait_ge(ctx_hi_done, e + 1)
            nc.vector.tensor_tensor(ctx_lo[:, e, :], ctx_raw[:, e, :], ctx_hi[:, e, :].bitcast(F32),
                                    ALU.subtract).then_inc(ctx_lo_done, 1)
        split(0, 0)
        dve.wait_ge(kv_scaled, 2)
        for g in range(GROUPS):
            dve.wait_ge(hi_done, g + 1)
            nc.vector.scalar_tensor_tensor(kv_lo[:, 0, g, :], ps[:, g, 0:GK], kv_scale[:],
                                           kv_hi[:, 0, g, :].bitcast(F32),
                                           ALU.mult, ALU.subtract).then_inc(lo_done, 1)

        dve.wait_ge(small_in, 16 * 10)
        dve.wait_ge(consts, 5)
        then_wait(nc.vector.tensor_scalar(nw2[:], nw[:], SCALE0 / SCALE, None, ALU.mult))
        then_wait(nc.vector.tensor_scalar(sel[:, 0:1], rowno[:], 2.0, None, ALU.is_lt))
        then_wait(nc.vector.tensor_scalar(sel[:, 1:2], rowno[:], 2.0, None, ALU.is_ge))
        then_wait(nc.vector.tensor_scalar(sel[:, 4:5], rowno[:], 0.0, None, ALU.is_equal))
        then_wait(nc.vector.tensor_scalar(sel[:, 2:3], rowno[:], 2.0, sel[:, 4:5], ALU.is_equal, ALU.add))
        then_wait(nc.vector.tensor_scalar(sel[:, 3:4], sel[:, 2:3], -1.0, 1.0, ALU.mult, ALU.add))
        then_wait(nc.vector.tensor_scalar(mrow[:], mrow[:], -1.0, 1.0, ALU.mult, ALU.add))
        then_wait(nc.vector.tensor_scalar(mrow[:], mrow[:], -SUPPRESS, None, ALU.mult))
        then_wait(nc.vector.tensor_copy(mhi[:], mrow[:]))
        then_wait(nc.vector.tensor_tensor(mlo[:], mrow[:], mhi[:].bitcast(F32), ALU.subtract))
        then_wait(nc.vector.tensor_scalar(mlo[:], mlo[:], sel[:, 3:4], None, ALU.mult))
        then_wait(nc.vector.scalar_tensor_tensor(penalty[:], mhi[:].bitcast(F32), sel[:, 2:3], mlo[:],
                                                 ALU.mult, ALU.add))
        then_wait(nc.vector.tensor_copy(tokf[:], tok[:]))
        then_wait(nc.vector.tensor_scalar(wrap[:], tokf[:], 0.0, float(SK), ALU.is_lt, ALU.mult))
        then_wait(nc.vector.tensor_tensor(tokf[:], tokf[:], wrap[:], ALU.add))
        then_wait(nc.vector.memset(key_is[:, 0, :].bitcast(F32), 0.0))
        for l in range(1, LAYERS):
            k = (l - 1) * 4
            then_wait(nc.vector.tensor_scalar(is_a[:], keyno[:], tokf[:, k:k + 1], None, ALU.is_equal))
            then_wait(nc.vector.scalar_tensor_tensor(is_a[:], keyno[:], tokf[:, k + 1:k + 2], is_a[:],
                                                     ALU.is_equal, ALU.max))
            then_wait(nc.vector.tensor_scalar(is_b[:], keyno[:], tokf[:, k + 2:k + 3], None, ALU.is_equal))
            then_wait(nc.vector.scalar_tensor_tensor(is_b[:], keyno[:], tokf[:, k + 3:k + 4], is_b[:],
                                                     ALU.is_equal, ALU.max))
            then_wait(nc.vector.tensor_scalar(other[:], is_b[:], -1.0, 1.0, ALU.mult, ALU.add))
            then_wait(nc.vector.tensor_tensor(is_a[:], is_a[:], other[:], ALU.mult))
            then_wait(nc.vector.tensor_scalar(is_a[:], is_a[:], sel[:, 0:1], None, ALU.mult))
            then_wait(nc.vector.scalar_tensor_tensor(is_b[:], is_b[:], sel[:, 1:2], is_a[:], ALU.mult, ALU.add))
            for s in range(GB):
                then_wait(nc.vector.tensor_copy(key_is[:, l, s * SK:(s + 1) * SK], is_b[:]))
        before = steps[0]
        NS = 4

        def mean_square(n):
            dve.wait_ge(summed, n + 1)
            nc.vector.tensor_scalar(ms[:], ps[:, 4, 0:RCH], 1.0 / C, EPS, ALU.mult, ALU.add).then_inc(ms_done, 1)

        def norm(n):
            def step(s, ins):
                ins.then_inc(dve_step, 1)
                dve.wait_ge(dve_step, n * NS + (before + s))
            dve.wait_ge(rooted, n + 1)
            step(1, nc.vector.reciprocal(inv[:], root[:]))
            step(2, nc.vector.scalar_tensor_tensor(corr[:], inv[:], -0.5, inv[:], ALU.mult, ALU.mult))
            step(3, nc.vector.tensor_tensor(corr[:], corr[:], ms[:], ALU.mult))
            step(4, nc.vector.scalar_tensor_tensor(inv2[:], corr[:], 1.5, inv[:], ALU.add, ALU.mult))
            for c in range(CT):
                last = nc.vector.scalar_tensor_tensor(xr[:, c, :], xr[:, c, :], nw2[:, c:c + 1], inv2[:],
                                                      ALU.mult, ALU.mult)
            last.then_inc(xn_done, 1)

        def job(j, m, g, chunks):
            n = j * GROUPS + g
            for mt in range(MT):
                if chunks and mt == 1:
                    mean_square(n)
                if chunks and mt == 4:
                    norm(n)
                tile_lo(n, mt, m)

        for kv in range(2):
            dve.wait_ge(kv_out[kv], 16 * 2 * HEADS)
        matrices(dve, split, job)

    @block.tensor
    def _(pe):
        def project(out, hi, lo, cols, keys):
            passes = [(a, b) for a, b in ((hi, ctx_hi), (hi, ctx_lo), (lo, ctx_hi))]
            for e in range(ET):
                for n, (a, b) in enumerate(passes):
                    last = nc.tensor.matmul(out, a[:, e, cols], b[:, e, keys], start=(e == 0 and n == 0),
                                            stop=(e == ET - 1 and n == 2))
            return last

        def split(j, m):
            pass

        def job(j, m, g, chunks):
            n = j * GROUPS + g
            for mt in range(MT):
                if mt == 0:
                    pe.wait_ge(w_lo_done, j + 1)
                if chunks and mt == 1:
                    pe.wait_ge(squared, n + 1)
                    for c in range(CT):
                        last = nc.tensor.matmul(ps[:, 4, 0:RCH], ones[:], xsq[:, c, :], start=(c == 0),
                                                stop=(c == CT - 1))
                    last.then_inc(summed, 1)
                pe.wait_ge(lo_done, n * MT + mt + 1)
                project(ps[:, mt % 4, 0:GK], w_hi[m], w_lo[m], slice(mt * P, (mt + 1) * P),
                        bass.ds(g * GK, GK)).then_inc(projected, 1)

        pe.wait_ge(ctx_lo_done, ET)
        for g in range(GROUPS):
            project(ps[:, g, 0:GK], w0_hi, w0_lo, slice(0, P), slice(g * GK, (g + 1) * GK)).then_inc(projected, 1)
        pe.wait_ge(consts, 5)
        matrices(pe, split, job)


def attend(nc, ctx, kv_dram, base_dram, query_dram, w_dram, ident, bo_sb, key_is, penalty, stored, outT):
    def sb(name, shape, dt):
        return ctx.enter_context(nc.sbuf_tensor(name, shape, dt))

    def sem(name):
        return ctx.enter_context(nc.semaphore(name))

    wh_hi = [sb(f"wh_hi{m}", [P, HH, C], F32R) for m in range(2)]
    wh_lo = [sb(f"wh_lo{m}", [P, HH, C], F32R) for m in range(2)]
    kv = [sb(f"kv{m}", [P, HH, GK], F32R) for m in range(2)]
    g_hi = sb("g_hi", [P, CT, GB, FLAT], F32R)
    g_lo = sb("g_lo", [P, CT, GB, FLAT], F32R)
    uT = sb("uT", [P, CT, GB, FLAT], F32)
    u_hi = sb("u_hi", [P, GB, FT, C], F32R)
    u_lo = sb("u_lo", [P, GB, FT, C], F32R)
    xq = [sb(f"xq{k}", [P, CT, SQ], F32) for k in range(2)]
    x_hi = [sb(f"x_hi{k}", [P, CT, SQ], F32R) for k in range(2)]
    x_lo = [sb(f"x_lo{k}", [P, CT, SQ], F32R) for k in range(2)]
    probs = [sb(f"probs{k}", [P, FLAT], F32) for k in range(3)]
    pT_hi = sb("pT_hi", [P, FT, SQ], F32R)
    pT_lo = sb("pT_lo", [P, FT, SQ], F32R)
    base = [sb(f"base{k}", [P, CT, SQ], F32) for k in range(2)]
    res = [sb(f"res{k}", [P, CT, SQ], F32) for k in range(2)]
    neg_max = [sb(f"neg_max{k}", [P, HH], F32) for k in range(2)]
    total = [sb(f"total{k}", [P, HH], F32) for k in range(3)]
    recip = [sb(f"recip{k}", [P, HH], F32) for k in range(3)]
    idle = sb("idle", [P, 4], F32)
    scores = ctx.enter_context(nc.psum_tensor("scores", [P, 4, 512], F32))
    work = ctx.enter_context(nc.psum_tensor("work", [P, 4, 512], F32))

    kv_in = [sem(f"kv_in{m}") for m in range(2)]
    wh_in = [sem(f"wh_in{m}") for m in range(2)]
    wh_hi_done = [sem(f"wh_hi_done{m}") for m in range(2)]
    wh_split = [sem(f"wh_split{m}") for m in range(2)]
    xq_in = [sem(f"xq_in{k}") for k in range(2)]
    base_in = [sem(f"base_in{k}") for k in range(2)]
    x_hi_done = sem("x_hi_done")
    x_split = sem("x_split")
    g_made = sem("g_made")
    g_hi_done = sem("g_hi_done")
    g_lo_done = sem("g_lo_done")
    uT_made = sem("uT_made")
    uT_act = sem("uT_act")
    uT_dve = sem("uT_dve")
    u_made = sem("u_made")
    u_hi_done = sem("u_hi_done")
    u_lo_done = sem("u_lo_done")
    scored = sem("scored")
    maxed = sem("maxed")
    exped = sem("exped")
    totalled = sem("totalled")
    recips = sem("recips")
    normed = sem("normed")
    turned = sem("turned")
    pT_hi_done = sem("pT_hi_done")
    pT_lo_done = sem("pT_lo_done")
    attended = sem("attended")
    res_done = sem("res_done")
    zeroed = sem("zeroed")

    block = ctx.enter_context(nc.Block())
    LATE = UNITS - GROUPS
    LAST_UNIT = UNITS - 1

    VALUES_AFTER = (2, 4, 6)
    G_PARTS = (range(0, 2), range(2, 9), range(9, N_G))

    def g_at(j):
        h, c = j // CT, j % CT
        return (slice(None), c, slice(None), slice(h * SK, (h + 1) * SK))

    def u_pair(s):
        b, t = s % GB, s // GB * 2
        if t == FT - 1:
            bs = slice(2 * b, 2 * b + 2)
            return [(2 * b, t), (2 * b + 1, t)], LAST, (slice(0, LAST), bs, t, slice(None))
        return [(b, t), (b, t + 1)], P, (slice(None), b, slice(t, t + 2), slice(None))

    def bank(j):
        return (j + 2) % 4

    def by_batch(ap):
        return ap.rearrange("p (b k) -> p b k", b=GB)

    @block.sync
    def _(sp):
        def load_kv(v, m, rows):
            for part in range(2):
                sp.dma_start(kv[m][part * HD:part * HD + rows, :, :].bitcast(F32),
                             kv_dram[v, m, part * HD:part * HD + rows, :].rearrange(
                                 "p (h n) -> p h n", h=HH)).then_inc(kv_in[m], 16)

        def load_weights(lh, m):
            for part in range(2):
                sp.dma_start(wh_lo[m][part * HD:(part + 1) * HD, :, :].bitcast(F32),
                             w_dram[lh, m].rearrange("p (h n) -> p h n", h=HH)).then_inc(wh_in[m], 16)

        def cols(b):
            return slice(b * SQ, (b + 1) * SQ)

        def load_queries(src, b):
            sp.dma_start(xq[b % 2][:], query_dram[src].rearrange("(c p) q -> p c q", p=P)[:, :, cols(b)]
                         ).then_inc(xq_in[b % 2], 16)

        base_rows = base_dram.rearrange("u c q -> (u c) q")

        def load_base(first_row, b):
            sp.dma_start(base[b % 2][:], base_rows[bass.ds(first_row, C), :].rearrange("(c p) q -> p c q", p=P)[:, :, cols(b)]
                         ).then_inc(base_in[b % 2], 16)

        def store(u, b, late):
            sp.wait_ge(res_done, u * GB + (b + 3))
            if late is None:
                for dst in (base_dram, query_dram):
                    sp.dma_start(dst[u + GROUPS].rearrange("(c p) q -> p c q", p=P)[:, :, cols(b)],
                                 res[b % 2][:]).then_inc(stored[b], 16)
            else:
                for c in range(CT):
                    sp.dma_start(outT[c * P:(c + 1) * P, bass.ds(late * GQ + b * SQ, SQ)],
                                 res[b % 2][:, c, :]).then_inc(stored[b], 16)

        def unit(u, src, next_src, next_rows, weights=None, late=None):
            stored_before = sp.snap(u * 32 + 32)
            base_row = sp.snap(u * C)
            for b in range(2, GB):
                sp.wait_ge(x_split, u * GB + (b - 1))
                sp.wait_ge(stored[b], stored_before)
                load_queries(src, b)
            if next_rows:
                sp.wait_ge(g_made, u * N_G + N_G)
                load_kv(u + 1, 0, next_rows)
            if weights is not None:
                load_weights(weights, 0)
            if next_rows:
                sp.wait_ge(uT_made, u * N_G + N_G)
                load_kv(u + 1, 1, next_rows)
            if weights is not None:
                load_weights(weights, 1)
            for b in range(2):
                sp.wait_ge(res_done, u * GB + (b + 1))
                sp.wait_ge(stored[b], stored_before)
                load_base(base_row, b)
            for b in range(2):
                if next_rows:
                    sp.wait_ge(x_split, u * GB + (b + 3))
                    sp.wait_ge(stored[b], stored_before)
                    load_queries(next_src, b)
                store(u, b, late)
                load_base(base_row, b + 2)
            for b in range(2, GB):
                store(u, b, late)

        sp.wait_ge(zeroed, 2)
        load_kv(0, 0, HD0)
        load_weights(0, 0)
        load_queries(0, 0)
        load_queries(0, 1)
        load_kv(0, 1, HD0)
        load_weights(0, 1)

        def layer(l, rows, next_rows, last=False):
            first, G3 = l * (2 * GROUPS), GROUPS - 1
            with sp.Fori(0, G3) as g:
                unit(first + g, first + g, first + (g + 1), rows)
            unit(first + G3, first + G3, first, rows, weights=l * 2 + 1)
            second = first + GROUPS
            with sp.Fori(0, G3) as g:
                unit(second + g, first + g, first + (g + 1), rows, late=g if last else None)
            if last:
                unit(second + G3, first + G3, None, 0, late=G3)
            else:
                unit(second + G3, first + G3, first + 2 * GROUPS, next_rows, weights=l * 2 + 2)

        layer(0, HD0, HD)
        with sp.Fori(1, LAYERS - 1) as l:
            layer(l, HD, HD)
        layer(LAYERS - 1, HD, 0, last=True)
        for b in range(GB):
            sp.wait_ge(stored[b], (UNITS + 1) * 32)

    def in_turn(eng, unit):
        with eng.Fori(0, HALVES - 1) as lh:
            with eng.Fori(0, GROUPS - 1) as g:
                unit(lh * GROUPS + g, lh, False)
            unit(lh * GROUPS + (GROUPS - 1), lh, True)
        with eng.Fori(0, GROUPS - 1) as g:
            unit(g + LATE, HALVES - 1, False)
        unit(LAST_UNIT, HALVES - 1, False)

    @block.scalar
    def _(act):
        def weights_hi(lh, m):
            act.wait_ge(wh_in[m], lh * 32 + 32)
            nc.scalar.copy(wh_hi[m][:], wh_lo[m][:].bitcast(F32)).then_inc(wh_hi_done[m], 1)

        def queries_hi(v, b):
            k = b % 2
            act.wait_ge(xq_in[k], v * 32 + 16 * (b // 2 + 1))
            if v is not FIRST or b > 1:
                act.wait_ge(scored, v * ITEMS + 2 * (b - 1))
            nc.scalar.copy(x_hi[k][:], xq[k][:]).then_inc(x_hi_done, 1)

        def tiles_hi(v, js):
            for j in js:
                act.wait_ge(g_made, v * N_G + (j + 1))
                nc.scalar.copy(g_hi[g_at(j)], by_batch(scores[:, j % 4, 0:GK])).then_inc(g_hi_done, 1)

        def tiles_uT(u, js):
            for j in js:
                act.wait_ge(uT_made, u * N_G + (j + 1))
                nc.scalar.copy(uT[g_at(j)], by_batch(work[:, bank(j), 0:GK])).then_inc(uT_act, 1)

        def exponents(u, i):
            act.wait_ge(maxed, u * ITEMS + (i + 1))
            if i != 2:
                act.wait_ge(turned, u * ITEMS + (i + 1 if i < 2 else i))
            k = i % 2
            for h in range(HH):
                last = nc.scalar.activation(
                    probs[i % 3][:, h * SK:(h + 1) * SK],
                    scores[:, 2 * k + h // 4, (h % 4) * SK:(h % 4 + 1) * SK],
                    ACT.Exp, bias=neg_max[k][:, h:h + 1])
            last.then_inc(exped, 1)

        def turned_hi(u, i):
            act.wait_ge(turned, u * ITEMS + (i + 3))
            q = slice(i % QT * P, (i % QT + 1) * P)
            nc.scalar.copy(pT_hi[:, 0:FT - 1, q], work[:, 0, :].rearrange("p (t q) -> p t q", q=P))
            nc.scalar.copy(pT_hi[0:LAST, FT - 1, q], work[0:LAST, 1, 0:P]).then_inc(pT_hi_done, 1)

        def unit(u, lh, weights):
            exponents(u, 0)
            tiles_uT(u, range(0, N_G // 2, 2))
            exponents(u, 1)
            queries_hi(u, 2)
            tiles_uT(u, range(N_G // 2, N_G, 2))
            for s in range(N_U):
                _, r, at = u_pair(s)
                act.wait_ge(u_made, u * N_U + (s + 1))
                nc.scalar.copy(u_hi[at], work[0:r, bank(s), :].rearrange("p (a n) -> p a n", a=2)).then_inc(u_hi_done, 1)
            for i in range(ITEMS):
                if i in VALUES_AFTER:
                    if i + 2 < ITEMS:
                        exponents(u, i + 2)
                    if i == 2:
                        queries_hi(u, 3)
                    elif u is not LAST_UNIT:
                        queries_hi(u + 1, i // 2 - 2)
                    if weights and i in (2, 4):
                        weights_hi(lh + 1, i // 2 - 1)
                    if i == 6 and u is not LAST_UNIT:
                        tiles_hi(u + 1, G_PARTS[0])
                    turned_hi(u, i)
                else:
                    if i == ITEMS - 1 and u is not LAST_UNIT:
                        tiles_hi(u + 1, G_PARTS[1])
                    turned_hi(u, i)
                    if i + 2 < ITEMS:
                        exponents(u, i + 2)
            if u is not LAST_UNIT:
                tiles_hi(u + 1, G_PARTS[2])

        act.wait_ge(zeroed, 3)
        nc.scalar.activation(idle[:, 3:4], idle[:, 2:3], ACT.Exp).then_inc(exped, 2)
        FIRST = 0
        weights_hi(0, 0)
        for b in range(2):
            queries_hi(FIRST, b)
        tiles_hi(0, range(N_G))
        weights_hi(0, 1)
        in_turn(act, unit)

    @block.vector
    def _(dve):
        def tiles_lo(v, js):
            for j in js:
                dve.wait_ge(g_hi_done, v * N_G + (j + 1))
                nc.vector.tensor_tensor(g_lo[g_at(j)], by_batch(scores[:, j % 4, 0:GK]),
                                        g_hi[g_at(j)].bitcast(F32), ALU.subtract).then_inc(g_lo_done, 1)

        def tiles_uT(u, js):
            for j in js:
                dve.wait_ge(uT_made, u * N_G + (j + 1))
                nc.vector.tensor_copy(uT[g_at(j)], by_batch(work[:, bank(j), 0:GK])).then_inc(uT_dve, 1)

        def maxima(u, i):
            k = i % 2
            dve.wait_ge(scored, u * ITEMS + (i + 1))
            nc.vector.tensor_reduce(neg_max[k][:].rearrange("p (a h) -> p a h", a=2),
                                    scores[:, 2 * k:2 * k + 2, 0:HFLAT].rearrange("p a (h n) -> p a h n", n=SK),
                                    AX.X, ALU.max, negate=True).then_inc(maxed, 1)

        def totals(u, i):
            k = i % 3
            dve.wait_ge(exped, u * ITEMS + (i + 3))
            nc.vector.tensor_reduce(total[k][:], probs[k][:].rearrange("p (h n) -> p h n", n=SK),
                                    AX.X, ALU.add).then_inc(totalled, 1)
            dve.wait_ge(totalled, u * ITEMS + (i + 1))
            nc.vector.reciprocal(recip[k][:], total[k][:]).then_inc(recips, 1)

        def turned_lo(u, i):
            dve.wait_ge(pT_hi_done, u * ITEMS + (i + 1))
            q = slice(i % QT * P, (i % QT + 1) * P)
            nc.vector.tensor_tensor(pT_lo[:, 0:FT - 1, q], work[:, 0, :].rearrange("p (t q) -> p t q", q=P),
                                    pT_hi[:, 0:FT - 1, q].bitcast(F32), ALU.subtract)
            nc.vector.tensor_tensor(pT_lo[0:LAST, FT - 1, q], work[0:LAST, 1, 0:P],
                                    pT_hi[0:LAST, FT - 1, q].bitcast(F32), ALU.subtract).then_inc(pT_lo_done, 1)

        def result(u, lh, b):
            k = b % 2
            dve.wait_ge(attended, u * GB + (b + 1))
            dve.wait_ge(base_in[k], u * 32 + 16 * (b // 2 + 1))
            dve.wait_ge(stored[(b + 2) % GB], u * 32 + 32 * (1 + b // 2))
            for c in range(CT):
                last = nc.vector.scalar_tensor_tensor(
                    res[k][:, c, :], work[:, 2 + k, c * SQ:(c + 1) * SQ], bo_sb[:, lh, c:c + 1],
                    base[k][:, c, :], ALU.add, ALU.add)
            last.then_inc(res_done, 1)

        def split_lo(lh, m):
            dve.wait_ge(wh_hi_done[m], lh + 1)
            nc.vector.tensor_tensor(wh_lo[m][:], wh_lo[m][:].bitcast(F32), wh_hi[m][:].bitcast(F32),
                                    ALU.subtract).then_inc(wh_split[m], 1)

        def unit(u, lh, weights):
            maxima(u, 0)
            maxima(u, 1)
            tiles_uT(u, range(1, N_G // 2, 2))
            totals(u, 0)
            maxima(u, 2)
            tiles_uT(u, range(N_G // 2 + 1, N_G, 2))
            totals(u, 1)
            for s in range(N_U):
                _, r, at = u_pair(s)
                dve.wait_ge(u_hi_done, u * N_U + (s + 1))
                nc.vector.tensor_tensor(u_lo[at], work[0:r, bank(s), :].rearrange("p (a n) -> p a n", a=2),
                                        u_hi[at].bitcast(F32), ALU.subtract).then_inc(u_lo_done, 1)
            for i in range(ITEMS):
                if 0 < i and i + 2 < ITEMS:
                    maxima(u, i + 2)
                if i == 1:
                    totals(u, 2)
                if i in VALUES_AFTER:
                    totals(u, i + 1)
                    if i + 2 < ITEMS:
                        totals(u, i + 2)
                    if i == 6 and u is not LAST_UNIT:
                        tiles_lo(u + 1, G_PARTS[0])
                    result(u, lh, i // 2 - 1)
                if i == ITEMS - 1 and u is not LAST_UNIT:
                    tiles_lo(u + 1, G_PARTS[1])
                turned_lo(u, i)
                if weights and i in (3, 5):
                    split_lo(lh + 1, i // 2 - 1)
            if u is not LAST_UNIT:
                tiles_lo(u + 1, G_PARTS[2])
            result(u, lh, GB - 1)

        for m in range(2):
            nc.vector.memset(kv[m][:].bitcast(F32), 0.0).then_inc(zeroed, 1)
        nc.vector.memset(idle[:, 0:1], 0.0).then_inc(pT_lo_done, 1)
        nc.vector.memset(idle[:, 1:2], 0.0).then_inc(res_done, 2)
        nc.vector.memset(idle[:, 2:3], 0.0).then_inc(zeroed, 1)
        split_lo(0, 0)
        tiles_lo(0, range(N_G))
        split_lo(0, 1)
        in_turn(dve, unit)

    @block.gpsimd
    def _(pool):
        def queries_lo(v, b):
            k = b % 2
            pool.wait_ge(x_hi_done, v * GB + (b + 1))
            nc.gpsimd.tensor_tensor(x_lo[k][:], xq[k][:], x_hi[k][:].bitcast(F32), ALU.subtract).then_inc(x_split, 1)

        def unit(u):
            for i in range(ITEMS):
                k = i % 3
                pool.wait_ge(recips, u * ITEMS + (i + 1))
                p3 = probs[k][:].rearrange("p (h n) -> p h n", n=SK)
                nc.gpsimd.tensor_tensor(p3, p3, recip[k][:].unsqueeze(2).to_broadcast((P, HH, SK)),
                                        ALU.mult).then_inc(normed, 1)
                if i in (0, 3):
                    queries_lo(u, i // 2 + 2)
                if i in (5, 7) and u is not LAST_UNIT:
                    queries_lo(u + 1, i // 2 - 2)

        for b in range(2):
            queries_lo(0, b)
        with pool.Fori(0, LAST_UNIT) as u:
            unit(u)
        unit(LAST_UNIT)

    @block.tensor
    def _(pe):
        def products(out, m, h, c):
            for n, w in enumerate((wh_hi, wh_lo)):
                last = nc.tensor.matmul(out, w[m][:, h, c * P:(c + 1) * P], kv[m][:, h, :],
                                        start=(n == 0), stop=(n == 1))
            return last

        def make_g(v, lh, js):
            for j in js:
                if j == 0:
                    pe.wait_ge(kv_in[0], v * 32 + 32)
                    pe.wait_ge(wh_split[0], lh + 1)
                if v is not FIRST and j in (0, 2):
                    pe.wait_ge(exped, v * ITEMS + (1 + j // 2))
                if j >= 4:
                    pe.wait_ge(g_lo_done, v * N_G + (j - 3))
                products(scores[:, j % 4, 0:GK], 0, j // CT, j % CT).then_inc(g_made, 1)

        def make_uT(u, lh, js):
            for j in js:
                if j == 0:
                    pe.wait_ge(kv_in[1], u * 32 + 32)
                    pe.wait_ge(wh_split[1], lh + 1)
                    pe.wait_ge(res_done, u * GB + 1)
                if j == 1:
                    pe.wait_ge(res_done, u * GB + 2)
                if j == 2:
                    pe.wait_ge(pT_lo_done, u * ITEMS + 1)
                if j >= 4:
                    pe.wait_ge(uT_dve if j % 2 else uT_act, u * (N_G // 2) + (j - 4) // 2 + 1)
                products(work[:, bank(j), 0:GK], 1, j // CT, j % CT).then_inc(uT_made, 1)

        def make_u(u):
            for s in range(N_U):
                tiles, r, _ = u_pair(s)
                if s < 4:
                    pe.wait_ge(uT_dve if s % 2 else uT_act, u * (N_G // 2) + (N_G - 4 + s) // 2 + 1)
                else:
                    pe.wait_ge(u_lo_done, u * N_U + (s - 3))
                for k, (b, t) in enumerate(tiles):
                    for c in range(CT):
                        last = nc.tensor.transpose(work[0:r, bank(s), (k * CT + c) * P:(k * CT + c + 1) * P],
                                                   uT[:, c, b, t * P:t * P + r], ident[:])
                last.then_inc(u_made, 1)

        def score(u, lh, i):
            b, q, k = i // QT, slice(i % QT * P, (i % QT + 1) * P), i % 2
            if i == 0:
                pe.wait_ge(g_lo_done, u * N_G + N_G)
            pe.wait_ge(x_split, u * GB + (b + 1))
            pe.wait_ge(exped, u * ITEMS + (i + 1))
            x = (x_hi[b % 2], x_lo[b % 2])
            out = [scores[:, 2 * k + a, 0:HFLAT] for a in range(2)]
            for c in range(CT):
                for n, (xp, gp) in enumerate(((x[0], g_hi), (x[0], g_lo), (x[1], g_hi))):
                    for a in range(2):
                        nc.tensor.matmul(out[a], xp[:, c, q], gp[:, c, b, a * HFLAT:(a + 1) * HFLAT],
                                         start=(c == 0 and n == 0), stop=False)
            for a in range(2):
                last = nc.tensor.matmul(out[a], penalty[:, q], key_is[:, lh // 2, :], start=False, stop=True)
            last.then_inc(scored, 1)

        def turn(u, i):
            if i == 0:
                pe.wait_ge(u_lo_done, u * N_U + (N_U - 2))
            pe.wait_ge(normed, u * ITEMS + (i + 1))
            pe.wait_ge(pT_lo_done, u * ITEMS + (i + 1))
            for t in range(FT):
                n = rows_of(t)
                out = work[:, 0, t * P:(t + 1) * P] if t < FT - 1 else work[0:n, 1, 0:P]
                last = nc.tensor.transpose(out, probs[i % 3][:, t * P:t * P + n], ident[:])
            last.then_inc(turned, 1)

        def attend_values(u, b):
            if b == 0:
                pe.wait_ge(u_lo_done, u * N_U + N_U)
            pe.wait_ge(pT_lo_done, u * ITEMS + (2 * b + 3))
            pe.wait_ge(res_done, u * GB + (b + 1))
            for c in range(CT):
                for t in range(FT):
                    r = rows_of(t)
                    for n, (up, pp) in enumerate(((u_hi, pT_hi), (u_hi, pT_lo), (u_lo, pT_hi))):
                        last = nc.tensor.matmul(work[:, 2 + b % 2, c * SQ:(c + 1) * SQ],
                                                up[0:r, b, t, c * P:(c + 1) * P], pp[0:r, t, :],
                                                start=(t == 0 and n == 0), stop=(t == FT - 1 and n == 2))
            last.then_inc(attended, 1)

        def unit(u, lh, weights):
            score(u, lh, 0)
            score(u, lh, 1)
            make_uT(u, lh, range(N_G // 2))
            score(u, lh, 2)
            make_uT(u, lh, range(N_G // 2, N_G))
            make_u(u)
            nxt = lh + 1 if weights else lh
            for i in range(ITEMS):
                if 0 < i and i + 2 < ITEMS:
                    score(u, lh, i + 2)
                if i + 2 >= ITEMS and u is not LAST_UNIT:
                    make_g(u + 1, nxt, G_PARTS[i + 2 - ITEMS])
                if i in VALUES_AFTER:
                    attend_values(u, i // 2 - 1)
                turn(u, i)
            if u is not LAST_UNIT:
                make_g(u + 1, nxt, G_PARTS[2])
            attend_values(u, GB - 1)

        nc.tensor.transpose(work[:, 0, 0:P], ident[:], ident[:]).then_inc(turned, 2)
        FIRST = 0
        make_g(FIRST, 0, range(N_G))
        in_turn(pe, unit)


def kernel(**inputs):
    import numpy as np
    import concourse.bacc as bacc
    from concourse.bass_utils import run_bass_kernel_spmd

    a = {k: np.asarray(v) for k, v in inputs.items()}
    L = [f"L{l}_xattn_" for l in range(LAYERS)]

    def heads_first(w, d):
        out = np.zeros((2, HD, HH, C), np.float32)
        out[:, :d] = w.reshape(2, HH, d, C).transpose(0, 2, 1, 3)
        return out.reshape(2, HD, HH * C)

    wheads = np.zeros((HALVES, 2, HD, HH * C), np.float32)
    bo = np.zeros((P, HALVES, CT), np.float32)
    for l in range(LAYERS):
        q, o, d = ("wq", "wo", HD0) if l == 0 else ("Wq", "Wo", HD)
        wheads[2 * l:2 * l + 2, 0] = heads_first(a[L[l] + q].T, d)
        wheads[2 * l:2 * l + 2, 1] = heads_first(a[L[l] + o], d)
        if l:
            bo[:, 2 * l, :] = a[L[l] + "bo"].reshape(CT, P).T
    arrays = {
        "xT": a["x"].reshape(B * SQ, C).T,
        "ctxT": a["ctx_2048"].reshape(B * SK, E).T,
        "wkv0": np.concatenate([a[L[0] + "wk"], a[L[0] + "wv"]], axis=1),
        "wkv": np.stack([a[L[l] + w] for l in range(1, LAYERS) for w in ("Wk", "Wv")]),
        "wheads": wheads,
        "normw": a[L[0] + "norm_w"].reshape(CT, P).T,
        "bo": bo.reshape(P, HALVES * CT),
        "masks": np.stack([a["mask_S_fk1"], a["mask_S_fk0"]]),
        "tokens": np.concatenate([a[L[l] + f"token_indices_{s}"] for l in range(1, LAYERS) for s in "AB"])[None, :],
    }
    arrays = {k: np.ascontiguousarray(v) for k, v in arrays.items()}
    nc = bacc.Bacc("TRN2", target_bir_lowering=False, num_devices=1)
    aps = {k: nc.dram_tensor(k, v.shape, mybir.dt.from_np(v.dtype), kind="ExternalInput").ap()
           for k, v in arrays.items()}
    outT = nc.dram_tensor("outT", (C, B * SQ), F32, kind="ExternalOutput").ap()
    build(nc, outT=outT, **aps)
    r = run_bass_kernel_spmd(nc, [arrays], core_ids=[0])
    return np.ascontiguousarray(r.results[0]["outT"].T).reshape(B, SQ, C)
```

```python
from contextlib import ExitStack

import concourse.bass as bass
from concourse import mybir

F32 = mybir.dt.float32
F32R = mybir.dt.float32r
I32 = mybir.dt.int32
ALU = mybir.AluOpType
ACT = mybir.ActivationFunctionType
AX = mybir.AxisListType

P = 128
LAYERS = 4
B, SQ, C = 16, 256, 256
SK, E = 77, 512
HEADS, HD = 16, 64
HD0, KVH0 = 16, 4
REP0 = HEADS // KVH0
CT, ET, QT = C // P, E // P, SQ // P
GB = 4
GROUPS = B // GB
GK, GQ = GB * SK, GB * SQ
HH = HEADS // 2
FLAT = HH * SK
HFLAT = FLAT // 2
FT = (FLAT + P - 1) // P
LAST = FLAT - (FT - 1) * P
HALVES = LAYERS * 2
UNITS = HALVES * GROUPS
ITEMS = GB * QT
MT = HEADS * HD // P
HMT = MT // 2
MATS = 2 * (LAYERS - 1)
N_G = HH * CT
N_U = GB * FT // 2
RCH = 512
RT = RCH // P
EPS = 1e-5
SUPPRESS = 20.0
SCALE = HD ** -0.5
SCALE0 = HD0 ** -0.5


def rows_of(t):
    return LAST if t == FT - 1 else P


def build(nc, xT, ctxT, wkv0, wkv, wheads, normw, bo, masks, tokens, outT):
    kv_dram = nc.dram_tensor("kv_dram", (UNITS, 2, P, HH * GK), F32, kind="Internal").ap()
    base_dram = nc.dram_tensor("base_dram", (UNITS, C, GQ), F32, kind="Internal").ap()
    query_dram = nc.dram_tensor("query_dram", (UNITS, C, GQ), F32, kind="Internal").ap()
    w_dram = nc.dram_tensor("w_dram", (HALVES, 2, HD, HH * C), F32, kind="Internal").ap()

    with ExitStack() as whole:
        def sb(name, shape, dt):
            return whole.enter_context(nc.sbuf_tensor(name, shape, dt))

        def sem(name):
            return whole.enter_context(nc.semaphore(name))

        ident = sb("ident", [P, P], F32)
        bo_sb = sb("bo_sb", [P, HALVES, CT], F32)
        key_is = sb("key_is", [4, LAYERS, GK], F32R)
        penalty = sb("penalty", [4, SQ], F32R)
        stored = [sem(f"stored{b}") for b in range(GB)]
        with ExitStack() as part:
            prepare(nc, part, xT, ctxT, wkv0, wkv, wheads, normw, bo, masks, tokens,
                    kv_dram, base_dram, query_dram, w_dram, ident, bo_sb, key_is, penalty, stored)
        with ExitStack() as part:
            attend(nc, part, kv_dram, base_dram, query_dram, w_dram,
                   ident, bo_sb, key_is, penalty, stored, outT)


def prepare(nc, ctx, xT, ctxT, wkv0, wkv, wheads, normw, bo, masks, tokens,
            kv_dram, base_dram, query_dram, w_dram, ident, bo_sb, key_is, penalty, stored):
    def sb(name, shape, dt):
        return ctx.enter_context(nc.sbuf_tensor(name, shape, dt))

    def sem(name):
        return ctx.enter_context(nc.semaphore(name))

    ctx_raw = sb("ctx_raw", [P, ET, B * SK], F32)
    ctx_hi = sb("ctx_hi", [P, ET, B * SK], F32R)
    ctx_lo = sb("ctx_lo", [P, ET, B * SK], F32R)
    w0_raw = sb("w0_raw", [P, ET, P], F32)
    w0_hi = sb("w0_hi", [P, ET, P], F32R)
    w0_lo = sb("w0_lo", [P, ET, P], F32R)
    w_raw = sb("w_raw", [P, ET, MT * P], F32)
    w_hi = [sb(f"w_hi{m}", [P, ET, MT * P], F32R) for m in range(2)]
    w_lo = [sb(f"w_lo{m}", [P, ET, MT * P], F32R) for m in range(2)]
    kv0_hi = sb("kv0_hi", [P, GROUPS, GK], F32R)
    kv0_lo = sb("kv0_lo", [P, GROUPS, GK], F32R)
    kv_hi = sb("kv_hi", [P, 2, HMT, GK], F32R)
    kv_lo = sb("kv_lo", [P, 2, HMT, GK], F32R)
    xr = [sb(f"xr{k}", [P, CT, RCH], F32) for k in range(2)]
    xn = sb("xn", [P, CT, RCH], F32)
    xsq = sb("xsq", [P, CT, RCH], F32)
    ms = sb("ms", [P, RT], F32)
    root = sb("root", [P, RT], F32)
    inv = sb("inv", [P, RT], F32)
    corr = sb("corr", [P, RT], F32)
    inv2 = sb("inv2", [P, RT], F32)
    diag = sb("diag", [P, RT, P], F32)
    ones = sb("ones", [P, P], F32)
    kv_scale = sb("kv_scale", [P, 1], F32)
    nw = sb("nw", [P, CT], F32)
    nw2 = sb("nw2", [P, CT], F32)
    tok = sb("tok", [4, (LAYERS - 1) * 4], I32)
    tokf = sb("tokf", [4, (LAYERS - 1) * 4], F32)
    wrap = sb("wrap", [4, (LAYERS - 1) * 4], F32)
    keyno = sb("keyno", [4, SK], F32)
    rowno = sb("rowno", [4, 1], F32)
    sel = sb("sel", [4, 8], F32)
    is_a = sb("is_a", [4, SK], F32)
    is_b = sb("is_b", [4, SK], F32)
    other = sb("other", [4, SK], F32)
    mrow = sb("mrow", [4, SQ], F32)
    mhi = sb("mhi", [4, SQ], F32R)
    mlo = sb("mlo", [4, SQ], F32)
    ps = ctx.enter_context(nc.psum_tensor("proj_ps", [P, 8, 512], F32))

    bo_in = sem("bo_in")
    ctx_in = [sem(f"ctx_in{e}") for e in range(ET)]
    w0_in = sem("w0_in")
    w_in = sem("w_in")
    xr_in = [sem(f"xr_in{k}") for k in range(2)]
    base_out = sem("base_out")
    xn_out = sem("xn_out")
    kv0_out = sem("kv0_out")
    kv_out = [sem(f"kv_out{h}") for h in range(2)]
    consts = sem("consts")
    ctx_hi_done = sem("ctx_hi_done")
    ctx_lo_done = sem("ctx_lo_done")
    w0_hi_done = sem("w0_hi_done")
    w_hi_done = sem("w_hi_done")
    w_lo_done = sem("w_lo_done")
    squared = sem("squared")
    summed = sem("summed")
    ms_done = sem("ms_done")
    rooted = sem("rooted")
    xn_done = sem("xn_done")
    projected = sem("projected")
    kv_scaled = sem("kv_scaled")
    hi_done = sem("hi_done")
    lo_done = sem("lo_done")
    dve_step = sem("dve_step")
    pool_step = sem("pool_step")
    diag_done = sem("diag_done")
    spread = sem("spread")

    table_steps = [0]

    x_v = xT.rearrange("(c p) q -> p c q", p=P)
    CPG = GQ // RCH
    CHUNKS = GROUPS * CPG

    block = ctx.enter_context(nc.Block())

    @block.gpsimd
    def _(pool):
        nc.gpsimd.memset(ones[:], 1.0).then_inc(consts, 1)
        nc.gpsimd.memset(ident[:], 0.0).then_inc(consts, 1)
        nc.gpsimd.iota(keyno[:], pattern=[[1, SK]], base=0, channel_multiplier=0,
                       allow_small_or_imprecise_dtypes=True).then_inc(consts, 1)
        nc.gpsimd.iota(rowno[:], pattern=[[0, 1]], base=0, channel_multiplier=1,
                       allow_small_or_imprecise_dtypes=True).then_inc(consts, 1)
        pool.wait_ge(consts, 4)
        nc.gpsimd.affine_select(out=ident[:], in_=ident[:], compare_op=ALU.not_equal, fill=1.0, base=0,
                                pattern=[[-1, P]], channel_multiplier=1).then_inc(consts, 1)

        def then_wait(ins):
            table_steps[0] += 1
            ins.then_inc(pool_step, 1)
            pool.wait_ge(pool_step, table_steps[0])

        for half in range(2):
            pool.wait_ge(kv_out[half], 64)
        pool.wait_ge(xn_out, 16)
        pool.wait_ge(consts, 5)
        then_wait(nc.gpsimd.tensor_scalar(nw2[:], nw[:], SCALE0 / SCALE, None, ALU.mult))
        then_wait(nc.gpsimd.tensor_scalar(sel[:, 0:1], rowno[:], 2.0, None, ALU.is_lt))
        then_wait(nc.gpsimd.tensor_scalar(sel[:, 1:2], rowno[:], 2.0, None, ALU.is_ge))
        then_wait(nc.gpsimd.tensor_scalar(sel[:, 4:5], rowno[:], 0.0, None, ALU.is_equal))
        then_wait(nc.gpsimd.tensor_scalar(sel[:, 2:3], rowno[:], 2.0, sel[:, 4:5], ALU.is_equal, ALU.add))
        then_wait(nc.gpsimd.tensor_scalar(sel[:, 3:4], sel[:, 2:3], -1.0, 1.0, ALU.mult, ALU.add))
        then_wait(nc.gpsimd.tensor_scalar(mrow[:], mrow[:], -1.0, 1.0, ALU.mult, ALU.add))
        then_wait(nc.gpsimd.tensor_scalar(mrow[:], mrow[:], -SUPPRESS, None, ALU.mult))
        then_wait(nc.gpsimd.tensor_copy(mhi[:], mrow[:]))
        then_wait(nc.gpsimd.tensor_tensor(mlo[:], mrow[:], mhi[:].bitcast(F32), ALU.subtract))
        then_wait(nc.gpsimd.tensor_scalar(mlo[:], mlo[:], sel[:, 3:4], None, ALU.mult))
        then_wait(nc.gpsimd.tensor_scalar(mrow[:], mhi[:].bitcast(F32), sel[:, 2:3], None, ALU.mult))
        then_wait(nc.gpsimd.tensor_tensor(penalty[:], mrow[:], mlo[:], ALU.add))
        then_wait(nc.gpsimd.tensor_copy(tokf[:], tok[:]))
        then_wait(nc.gpsimd.tensor_scalar(wrap[:], tokf[:], 0.0, float(SK), ALU.is_lt, ALU.mult))
        then_wait(nc.gpsimd.tensor_tensor(tokf[:], tokf[:], wrap[:], ALU.add))
        then_wait(nc.gpsimd.memset(key_is[:, 0, :].bitcast(F32), 0.0))
        for l in range(1, LAYERS):
            k = (l - 1) * 4
            then_wait(nc.gpsimd.tensor_scalar(is_a[:], keyno[:], tokf[:, k:k + 1], None, ALU.is_equal))
            then_wait(nc.gpsimd.tensor_scalar(other[:], keyno[:], tokf[:, k + 1:k + 2], None, ALU.is_equal))
            then_wait(nc.gpsimd.tensor_tensor(is_a[:], is_a[:], other[:], ALU.add))
            then_wait(nc.gpsimd.tensor_scalar(is_a[:], is_a[:], 1.0, None, ALU.min))
            then_wait(nc.gpsimd.tensor_scalar(is_b[:], keyno[:], tokf[:, k + 2:k + 3], None, ALU.is_equal))
            then_wait(nc.gpsimd.tensor_scalar(other[:], keyno[:], tokf[:, k + 3:k + 4], None, ALU.is_equal))
            then_wait(nc.gpsimd.tensor_tensor(is_b[:], is_b[:], other[:], ALU.add))
            then_wait(nc.gpsimd.tensor_scalar(is_b[:], is_b[:], 1.0, None, ALU.min))
            then_wait(nc.gpsimd.tensor_scalar(other[:], is_b[:], -1.0, 1.0, ALU.mult, ALU.add))
            then_wait(nc.gpsimd.tensor_tensor(is_a[:], is_a[:], other[:], ALU.mult))
            then_wait(nc.gpsimd.tensor_scalar(is_a[:], is_a[:], sel[:, 0:1], None, ALU.mult))
            then_wait(nc.gpsimd.tensor_scalar(is_b[:], is_b[:], sel[:, 1:2], None, ALU.mult))
            then_wait(nc.gpsimd.tensor_tensor(is_b[:], is_b[:], is_a[:], ALU.add))
            for s in range(GB):
                then_wait(nc.gpsimd.tensor_copy(key_is[:, l, s * SK:(s + 1) * SK], is_b[:]))

        pool.wait_ge(lo_done, GROUPS)
        for kv in range(2):
            for g in range(KVH0):
                r, h = kv * HD + g * HD0, g * REP0
                u, s = (h // HH) * GROUPS, h % HH
                for part, src in enumerate((kv0_hi, kv0_lo)):
                    for rep in range(REP0):
                        pool.dma_start(
                            kv_dram[u:u + GROUPS, kv, part * HD:part * HD + HD0,
                                    (s + rep) * GK:(s + rep + 1) * GK].rearrange("u p n -> p u n"),
                            src[r:r + HD0, :, :].bitcast(F32)).then_inc(kv0_out, 16)

    @block.sync
    def _(sp):
        sp.dma_start(w0_raw[:], wkv0.rearrange("(e p) n -> p e n", p=P)).then_inc(w0_in, 16)
        for e in range(ET):
            sp.dma_start(ctx_raw[:, e, :], ctxT[e * P:(e + 1) * P, :]).then_inc(ctx_in[e], 16)
        sp.dma_start(w_raw[:], wkv[0].rearrange("(e p) n -> p e n", p=P)).then_inc(w_in, 16)
        for k in range(2):
            sp.dma_start(xr[k][:], x_v[:, :, k * RCH:(k + 1) * RCH]).then_inc(xr_in[k], 16)
        sp.dma_start(nw[:], normw).then_inc(xn_out, 16)
        sp.dma_start(bo_sb[:].rearrange("p l c -> p (l c)"), bo).then_inc(bo_in, 16)
        for r in range(4):
            sp.dma_start(mrow[r:r + 1, :], masks[r // 2:r // 2 + 1, :]).then_inc(kv_out[0], 16)
            sp.dma_start(tok[r:r + 1, :], tokens).then_inc(kv_out[1], 16)

        def stores(j, m, g, half):
            sp.wait_ge(lo_done, (j * GROUPS + g) * MT + (GROUPS + HMT * (half + 1)))
            u = (j - m) * GROUPS + g + (2 + half) * GROUPS
            for part, src in enumerate((kv_hi, kv_lo)):
                for odd in range(2):
                    sp.dma_start(
                        kv_dram[u, m, part * HD:(part + 1) * HD, :].rearrange(
                            "p (t s n) -> p t s n", t=HMT, s=2)[:, :, odd, :],
                        src[odd * HD:(odd + 1) * HD, half, :, :].bitcast(F32)
                    ).then_inc(kv_out[half], 16)

        def chunk(n):
            def place(dram):
                return dram[n // CPG].rearrange("(c p) q -> p c q", p=P)[:, :, n % CPG * RCH:(n % CPG + 1) * RCH]
            sp.wait_ge(xr_in[n % 2], 16 * (n // 2 + 1))
            sp.dma_start(place(base_dram), xr[n % 2][:]).then_inc(base_out, 16)
            sp.wait_ge(xn_done, n + 1)
            sp.dma_start(place(query_dram), xn[:]).then_inc(xn_out, 16)
            if n + 2 < CHUNKS:
                sp.wait_ge(base_out, 16 * (n + 1))
                sp.dma_start(xr[n % 2][:], x_v[:, :, (n + 2) * RCH:(n + 3) * RCH]).then_inc(xr_in[n % 2], 16)

        def matrix(j, m, chunks):
            following = (j + 1) % MATS if chunks else sp.snap((j + 1) % MATS)
            sp.wait_ge(w_lo_done, j * ET + ET)
            sp.dma_start(w_raw[:], wkv[following].rearrange("(e p) n -> p e n", p=P)).then_inc(w_in, 16)
            if chunks:
                for g in range(GROUPS):
                    stores(j, m, g, 0)
                    chunk(j * GROUPS + g)
                    stores(j, m, g, 1)
            else:
                with sp.Fori(0, GROUPS) as g:
                    for half in range(2):
                        stores(j, m, g, half)

        for m in range(2):
            matrix(m, m, True)
        with sp.Fori(1, LAYERS - 1) as l:
            for m in range(2):
                matrix(l * 2 + m, m, False)
        for half in range(2):
            sp.wait_ge(kv_out[half], 16 * (4 + 4 * MATS * GROUPS))
        sp.wait_ge(kv0_out, 16 * 4 * HEADS)
        for b in range(GB):
            sp.wait_ge(stored[b], 32)
        sp.wait_ge(xn_out, 16 * (CHUNKS + 1))
        sp.wait_ge(base_out, 16 * CHUNKS)
        sp.wait_ge(bo_in, 16)
        sp.wait_ge(w_in, 16 * (MATS + 1))

    def matrices(eng, split, job):
        def matrix(j, m, chunks):
            if chunks:
                job(j, m, 0, True)
                job(j, m, 1, True)
            else:
                with eng.Fori(0, 2) as g:
                    job(j, m, g, False)
            job(j, m, 2, chunks, split)
            job(j, m, 3, chunks)
        for m in range(2):
            matrix(m, m, True)
        with eng.Fori(1, LAYERS - 1) as l:
            for m in range(2):
                matrix(l * 2 + m, m, False)

    @block.scalar
    def _(act):
        def split(j, m, e):
            if e == 0:
                act.wait_ge(w_in, j * 16 + 16)
            nc.scalar.copy(w_hi[m][:, e, :], w_raw[:, e, :]).then_inc(w_hi_done, 1)

        def job(j, m, g, chunks, split=None):
            n = j * GROUPS + g
            for mt in range(MT):
                if chunks and mt == 1:
                    act.wait_ge(xr_in[n % 2], 16 * (n // 2 + 1))
                    nc.scalar.activation(xsq[:], xr[n % 2][:], ACT.Square).then_inc(squared, 1)
                if chunks and mt == 3:
                    act.wait_ge(ms_done, n + 1)
                    nc.scalar.activation(root[:], ms[:], ACT.Sqrt).then_inc(rooted, 1)
                act.wait_ge(projected, n * MT + (GROUPS + mt + 1))
                if mt % HMT == 0:
                    act.wait_ge(kv_out[mt // HMT], n * 64 + 64)
                dst, src = kv_hi[:, mt // HMT, mt % HMT, :], ps[:, mt % 4, 0:GK]
                if m == 0:
                    ins = nc.scalar.mul(dst, src, SCALE)
                else:
                    ins = nc.scalar.copy(dst, src)
                ins.then_inc(hi_done, 1)
                if split and mt % 2:
                    split(j + 1, 1 - m, mt // 2)
            if not chunks and split:
                for k in range(2):
                    lh = (j - 2) * 2 + k
                    act.dma_start(w_dram[lh], wheads[lh]).then_inc(stored[2 * m + k], 16)

        act.wait_ge(w0_in, 16)
        nc.scalar.copy(w0_hi[:], w0_raw[:]).then_inc(w0_hi_done, 1)
        for e in range(ET):
            act.wait_ge(ctx_in[e], 16)
            nc.scalar.copy(ctx_hi[:, e, :], ctx_raw[:, e, :]).then_inc(ctx_hi_done, 1)
        for e in range(ET):
            split(0, 0, e)
        act.wait_ge(kv_scaled, 1)
        for g in range(GROUPS):
            act.wait_ge(projected, g + 1)
            nc.scalar.mul(kv0_hi[:, g, :], ps[:, g, 0:GK], kv_scale[:]).then_inc(hi_done, 1)
        matrices(act, split, job)

    @block.vector
    def _(dve):
        def split(j, m, e):
            dve.wait_ge(w_hi_done, j * ET + (e + 1))
            nc.vector.tensor_tensor(w_lo[m][:, e, :], w_raw[:, e, :], w_hi[m][:, e, :].bitcast(F32),
                                    ALU.subtract).then_inc(w_lo_done, 1)

        def tile_lo(n, mt, m):
            dve.wait_ge(hi_done, n * MT + (GROUPS + mt + 1))
            dst, src = kv_lo[:, mt // HMT, mt % HMT, :], ps[:, mt % 4, 0:GK]
            hi = kv_hi[:, mt // HMT, mt % HMT, :].bitcast(F32)
            if m == 0:
                ins = nc.vector.scalar_tensor_tensor(dst, src, SCALE, hi, ALU.mult, ALU.subtract)
            else:
                ins = nc.vector.tensor_tensor(dst, src, hi, ALU.subtract)
            ins.then_inc(lo_done, 1)

        nc.vector.memset(kv_scale[0:HD, :], SCALE).then_inc(kv_scaled, 1)
        nc.vector.memset(kv_scale[HD:P, :], 1.0).then_inc(kv_scaled, 1)
        dve.wait_ge(w0_hi_done, 1)
        nc.vector.tensor_tensor(w0_lo[:], w0_raw[:], w0_hi[:].bitcast(F32), ALU.subtract)
        for e in range(ET):
            dve.wait_ge(ctx_hi_done, e + 1)
            nc.vector.tensor_tensor(ctx_lo[:, e, :], ctx_raw[:, e, :], ctx_hi[:, e, :].bitcast(F32),
                                    ALU.subtract).then_inc(ctx_lo_done, 1)
        for e in range(ET):
            split(0, 0, e)
        dve.wait_ge(kv_scaled, 2)
        for g in range(GROUPS):
            dve.wait_ge(hi_done, g + 1)
            nc.vector.scalar_tensor_tensor(kv0_lo[:, g, :], ps[:, g, 0:GK], kv_scale[:],
                                           kv0_hi[:, g, :].bitcast(F32),
                                           ALU.mult, ALU.subtract).then_inc(lo_done, 1)

        NS = 4

        def mean_square(n):
            dve.wait_ge(summed, n + 1)
            nc.vector.tensor_scalar(ms[:], ps[:, 4, 0:RT], 1.0 / C, EPS, ALU.mult, ALU.add).then_inc(ms_done, 1)

        def norm(n):
            def step(s, ins):
                ins.then_inc(dve_step, 1)
                dve.wait_ge(dve_step, n * NS + s)
            dve.wait_ge(rooted, n + 1)
            step(1, nc.vector.reciprocal(inv[:], root[:]))
            step(2, nc.vector.scalar_tensor_tensor(corr[:], inv[:], -0.5, inv[:], ALU.mult, ALU.mult))
            step(3, nc.vector.tensor_tensor(corr[:], corr[:], ms[:], ALU.mult))
            step(4, nc.vector.scalar_tensor_tensor(inv2[:], corr[:], 1.5, inv[:], ALU.add, ALU.mult))
            for t in range(RT):
                last = nc.vector.tensor_scalar(diag[:, t, :], ident[:], inv2[:, t:t + 1], None, ALU.mult)
            last.then_inc(diag_done, 1)

        def scaled(n):
            dve.wait_ge(spread, n + 1)
            dve.wait_ge(xn_out, n * 16 + 16)
            for c in range(CT):
                last = nc.vector.scalar_tensor_tensor(xn[:, c, :], xr[n % 2][:, c, :], nw2[:, c:c + 1],
                                                      ps[:, 5, 0:RCH], ALU.mult, ALU.mult)
            last.then_inc(xn_done, 1)

        def job(j, m, g, chunks, split=None):
            n = j * GROUPS + g
            for mt in range(MT):
                if chunks and mt == 2:
                    mean_square(n)
                tile_lo(n, mt, m)
                if split and mt % 2:
                    split(j + 1, 1 - m, mt // 2)
                if chunks and mt == 3:
                    norm(n)
                if chunks and mt == 6:
                    scaled(n)

        dve.wait_ge(consts, 5)
        dve.wait_ge(pool_step, 1)
        matrices(dve, split, job)

    @block.tensor
    def _(pe):
        def project(out, hi, lo, cols, keys):
            passes = [(a, b) for a, b in ((hi, ctx_hi), (hi, ctx_lo), (lo, ctx_hi))]
            for e in range(ET):
                for n, (a, b) in enumerate(passes):
                    last = nc.tensor.matmul(out, a[:, e, cols], b[:, e, keys], start=(e == 0 and n == 0),
                                            stop=(e == ET - 1 and n == 2))
            return last

        def job(j, m, g, chunks, split=None):
            n = j * GROUPS + g
            for mt in range(MT):
                if mt == 0:
                    pe.wait_ge(w_lo_done, j * ET + ET)
                if chunks and mt == 2:
                    pe.wait_ge(squared, n + 1)
                    for t in range(RT):
                        for c in range(CT):
                            last = nc.tensor.matmul(ps[:, 4, t:t + 1], xsq[:, c, t * P:(t + 1) * P],
                                                    ones[:, 0:1], start=(c == 0), stop=(c == CT - 1))
                    last.then_inc(summed, 1)
                if chunks and mt == 6:
                    pe.wait_ge(diag_done, n + 1)
                    nc.tensor.matmul(ps[:, 5, 0:RCH], ones[:], diag[:].rearrange("p t q -> p (t q)"),
                                     start=True, stop=True).then_inc(spread, 1)
                pe.wait_ge(lo_done, n * MT + mt + 1)
                project(ps[:, mt % 4, 0:GK], w_hi[m], w_lo[m], slice(mt * P, (mt + 1) * P),
                        bass.ds(g * GK, GK)).then_inc(projected, 1)

        pe.wait_ge(ctx_lo_done, ET)
        for g in range(GROUPS):
            project(ps[:, g, 0:GK], w0_hi, w0_lo, slice(0, P), slice(g * GK, (g + 1) * GK)).then_inc(projected, 1)
        pe.wait_ge(consts, 5)
        matrices(pe, None, job)


def attend(nc, ctx, kv_dram, base_dram, query_dram, w_dram, ident, bo_sb, key_is, penalty, stored, outT):
    def sb(name, shape, dt):
        return ctx.enter_context(nc.sbuf_tensor(name, shape, dt))

    def sem(name):
        return ctx.enter_context(nc.semaphore(name))

    wh_hi = [sb(f"wh_hi{m}", [P, HH, C], F32R) for m in range(2)]
    wh_lo = [sb(f"wh_lo{m}", [P, HH, C], F32R) for m in range(2)]
    kv = [sb(f"kv{m}", [P, HH, GK], F32R) for m in range(2)]
    g_hi = sb("g_hi", [P, CT, GB, FLAT], F32R)
    g_lo = sb("g_lo", [P, CT, GB, FLAT], F32R)
    uT = sb("uT", [P, CT, GB, FLAT], F32)
    u_hi = sb("u_hi", [P, GB, FT, C], F32R)
    u_lo = sb("u_lo", [P, GB, FT, C], F32R)
    xq = [sb(f"xq{k}", [P, CT, SQ], F32) for k in range(2)]
    x_hi = [sb(f"x_hi{k}", [P, CT, SQ], F32R) for k in range(2)]
    x_lo = [sb(f"x_lo{k}", [P, CT, SQ], F32R) for k in range(2)]
    probs = [sb(f"probs{k}", [P, FLAT], F32) for k in range(3)]
    pT_hi = [sb(f"pT_hi{k}", [P, FT, SQ], F32R) for k in range(2)]
    pT_lo = [sb(f"pT_lo{k}", [P, FT, SQ], F32R) for k in range(2)]
    base = [sb(f"base{k}", [P, CT, SQ], F32) for k in range(2)]
    res = [sb(f"res{k}", [P, CT, SQ], F32) for k in range(2)]
    neg_max = [sb(f"neg_max{k}", [P, HH], F32) for k in range(2)]
    total = [sb(f"total{k}", [P, HH], F32) for k in range(3)]
    recip = [sb(f"recip{k}", [P, HH], F32) for k in range(3)]
    idle = sb("idle", [P, 4], F32)
    scores = ctx.enter_context(nc.psum_tensor("scores", [P, 4, 512], F32))
    work = ctx.enter_context(nc.psum_tensor("work", [P, 4, 512], F32))

    kv_in = [sem(f"kv_in{m}") for m in range(2)]
    wh_in = [sem(f"wh_in{m}") for m in range(2)]
    wh_hi_done = [sem(f"wh_hi_done{m}") for m in range(2)]
    wh_split = [sem(f"wh_split{m}") for m in range(2)]
    xq_in = [sem(f"xq_in{k}") for k in range(2)]
    base_in = [sem(f"base_in{k}") for k in range(2)]
    x_hi_done = sem("x_hi_done")
    x_split = sem("x_split")
    g_made = sem("g_made")
    g_hi_done = sem("g_hi_done")
    g_lo_done = sem("g_lo_done")
    uT_made = sem("uT_made")
    uT_act = sem("uT_act")
    uT_dve = sem("uT_dve")
    u_made = sem("u_made")
    u_hi_done = sem("u_hi_done")
    u_lo_done = sem("u_lo_done")
    scored = sem("scored")
    maxed = sem("maxed")
    exped = sem("exped")
    totalled = sem("totalled")
    recips = sem("recips")
    normed = sem("normed")
    turned = sem("turned")
    pT_hi_done = sem("pT_hi_done")
    pT_lo_done = sem("pT_lo_done")
    attended = sem("attended")
    res_done = sem("res_done")
    zeroed = sem("zeroed")

    block = ctx.enter_context(nc.Block())
    LATE = UNITS - GROUPS
    LAST_UNIT = UNITS - 1

    G_PARTS = [range(0, 2), range(2, 6), range(6, 8), range(8, 12), range(12, N_G)]

    def g_at(j):
        h, c = j // CT, j % CT
        return (slice(None), c, slice(None), slice(h * SK, (h + 1) * SK))

    def u_pair(s):
        b, t = s % GB, s // GB * 2
        if t == FT - 1:
            bs = slice(2 * b, 2 * b + 2)
            return [(2 * b, t), (2 * b + 1, t)], LAST, (slice(0, LAST), bs, t, slice(None))
        return [(b, t), (b, t + 1)], P, (slice(None), b, slice(t, t + 2), slice(None))

    def bank(j):
        return j % 4 if j < N_U - 2 else 2 + j % 2

    def by_batch(ap):
        return ap.rearrange("p (b k) -> p b k", b=GB)

    @block.sync
    def _(sp):
        def load_kv(v, m, rows):
            for part in range(2):
                sp.dma_start(kv[m][part * HD:part * HD + rows, :, :].bitcast(F32),
                             kv_dram[v, m, part * HD:part * HD + rows, :].rearrange(
                                 "p (h n) -> p h n", h=HH)).then_inc(kv_in[m], 16)

        def load_weights(lh, m):
            for part in range(2):
                sp.dma_start(wh_lo[m][part * HD:(part + 1) * HD, :, :].bitcast(F32),
                             w_dram[lh, m].rearrange("p (h n) -> p h n", h=HH)).then_inc(wh_in[m], 16)

        def cols(b):
            return slice(b * SQ, (b + 1) * SQ)

        def load_queries(src, b):
            sp.dma_start(xq[b % 2][:], query_dram[src].rearrange("(c p) q -> p c q", p=P)[:, :, cols(b)]
                         ).then_inc(xq_in[b % 2], 16)

        base_rows = base_dram.rearrange("u c q -> (u c) q")

        def load_base(first_row, b):
            sp.dma_start(base[b % 2][:], base_rows[bass.ds(first_row, C), :].rearrange(
                "(c p) q -> p c q", p=P)[:, :, cols(b)]).then_inc(base_in[b % 2], 16)

        def store(u, b, late, queries):
            sp.wait_ge(res_done, u * GB + (b + 3))
            if late is None and queries:
                for dst in (base_dram, query_dram):
                    sp.dma_start(dst[u + GROUPS].rearrange("(c p) q -> p c q", p=P)[:, :, cols(b)],
                                 res[b % 2][:]).then_inc(stored[b], 16)
            elif late is None:
                for c in range(CT):
                    sp.dma_start(base_dram[u + GROUPS, c * P:(c + 1) * P, cols(b)],
                                 res[b % 2][:, c, :]).then_inc(stored[b], 16)
            else:
                for c in range(CT):
                    sp.dma_start(outT[c * P:(c + 1) * P, bass.ds(late * GQ + b * SQ, SQ)],
                                 res[b % 2][:, c, :]).then_inc(stored[b], 16)

        def unit(u, src, next_src, next_rows, weights=None, late=None, queries=False):
            stored_before = sp.snap(u * 32 + 32)
            base_row = sp.snap(u * C)
            for b in range(2, GB):
                sp.wait_ge(x_split, u * GB + (b - 1))
                sp.wait_ge(stored[b], stored_before)
                load_queries(src, b)
            if next_rows:
                sp.wait_ge(g_made, u * N_G + N_G)
                load_kv(u + 1, 0, next_rows)
            if weights is not None:
                load_weights(weights, 0)
            if next_rows:
                sp.wait_ge(uT_made, u * N_G + N_G)
                load_kv(u + 1, 1, next_rows)
            if weights is not None:
                load_weights(weights, 1)
            for b in range(2):
                sp.wait_ge(res_done, u * GB + (b + 1))
                sp.wait_ge(stored[b], stored_before)
                load_base(base_row, b)
            for b in range(2):
                if next_rows:
                    sp.wait_ge(x_split, u * GB + (b + 3))
                    sp.wait_ge(stored[b], stored_before)
                    load_queries(next_src, b)
                store(u, b, late, queries)
                load_base(base_row, b + 2)
            for b in range(2, GB):
                store(u, b, late, queries)

        load_weights(0, 0)
        load_queries(0, 0)
        load_queries(0, 1)
        for m in range(2):
            sp.wait_ge(zeroed, m + 2)
            load_kv(0, m, HD0)
        load_weights(0, 1)

        def layer(l, rows, next_rows, last=False):
            first, G3 = l * (2 * GROUPS), GROUPS - 1
            with sp.Fori(0, G3) as g:
                unit(first + g, first + g, first + (g + 1), rows)
            unit(first + G3, first + G3, first, rows, weights=l * 2 + 1)
            second = first + GROUPS
            with sp.Fori(0, G3) as g:
                unit(second + g, first + g, first + (g + 1), rows, late=g if last else None, queries=True)
            if last:
                unit(second + G3, first + G3, None, 0, late=G3)
            else:
                unit(second + G3, first + G3, first + 2 * GROUPS, next_rows, weights=l * 2 + 2, queries=True)

        layer(0, HD0, HD)
        with sp.Fori(1, LAYERS - 1) as l:
            layer(l, HD, HD)
        layer(LAYERS - 1, HD, 0, last=True)
        for b in range(GB):
            sp.wait_ge(stored[b], (UNITS + 1) * 32)

    def in_turn(eng, unit):
        with eng.Fori(0, HALVES - 1) as lh:
            with eng.Fori(0, GROUPS - 1) as g:
                unit(lh * GROUPS + g, lh, False)
            unit(lh * GROUPS + (GROUPS - 1), lh, True)
        with eng.Fori(0, GROUPS - 1) as g:
            unit(g + LATE, HALVES - 1, False)
        unit(LAST_UNIT, HALVES - 1, False)

    @block.scalar
    def _(act):
        def weights_hi(lh, m):
            act.wait_ge(wh_in[m], lh * 32 + 32)
            nc.scalar.copy(wh_hi[m][:], wh_lo[m][:].bitcast(F32)).then_inc(wh_hi_done[m], 1)

        def queries_hi(v, b):
            k = b % 2
            act.wait_ge(xq_in[k], v * 32 + 16 * (b // 2 + 1))
            if v is not FIRST or b > 1:
                act.wait_ge(scored, v * ITEMS + 2 * (b - 1))
            nc.scalar.copy(x_hi[k][:], xq[k][:]).then_inc(x_hi_done, 1)

        def tiles_hi(v, js):
            for j in js:
                act.wait_ge(g_made, v * N_G + (j + 1))
                nc.scalar.copy(g_hi[g_at(j)], by_batch(scores[:, j % 4, 0:GK])).then_inc(g_hi_done, 1)

        def tiles_uT(u, js):
            for j in js:
                act.wait_ge(uT_made, u * N_G + (j + 1))
                nc.scalar.copy(uT[g_at(j)], by_batch(work[:, j % 4, 0:GK])).then_inc(uT_act, 1)

        def exponents(u, i):
            act.wait_ge(maxed, u * ITEMS + (i + 1))
            if i != 2:
                act.wait_ge(turned, u * ITEMS + (i + 1 if i < 2 else i))
            k = i % 2
            for h in range(HH):
                last = nc.scalar.activation(
                    probs[i % 3][:, h * SK:(h + 1) * SK],
                    scores[:, 2 * k + h // 4, (h % 4) * SK:(h % 4 + 1) * SK],
                    ACT.Exp, bias=neg_max[k][:, h:h + 1])
            last.then_inc(exped, 1)

        def pairs_hi(u, pairs):
            for s in pairs:
                _, r, at = u_pair(s)
                act.wait_ge(u_made, u * N_U + (s + 1))
                nc.scalar.copy(u_hi[at], work[0:r, bank(s), :].rearrange("p (a n) -> p a n", a=2)).then_inc(u_hi_done, 1)

        def turned_hi(u, i):
            act.wait_ge(turned, u * ITEMS + (i + 3))
            q = slice(i % QT * P, (i % QT + 1) * P)
            hi = pT_hi[i // QT % 2]
            nc.scalar.copy(hi[:, 0:FT - 1, q], work[:, 0, :].rearrange("p (t q) -> p t q", q=P))
            nc.scalar.copy(hi[0:LAST, FT - 1, q], work[0:LAST, 1, 0:P]).then_inc(pT_hi_done, 1)

        def unit(u, lh, weights):
            exponents(u, 0)
            tiles_uT(u, range(0, N_G // 2, 2))
            exponents(u, 1)
            queries_hi(u, 2)
            tiles_uT(u, range(N_G // 2, N_G, 2))
            pairs_hi(u, range(N_U - 2))
            another = u is not LAST_UNIT
            for i in range(ITEMS):
                turned_hi(u, i)
                if i + 2 < ITEMS:
                    exponents(u, i + 2)
                if i == 0:
                    pairs_hi(u, range(N_U - 2, N_U))
                if weights and i in (2, 3):
                    weights_hi(lh + 1, i - 2)
                if i == 1:
                    queries_hi(u, 3)
                elif i == 4 and another:
                    queries_hi(u + 1, 0)
                if another and i == ITEMS - 2:
                    queries_hi(u + 1, 1)
                if another and i >= ITEMS - 3:
                    tiles_hi(u + 1, G_PARTS[i - (ITEMS - 3)])
            if another:
                tiles_hi(u + 1, G_PARTS[3])
                tiles_hi(u + 1, G_PARTS[4])

        act.wait_ge(zeroed, 1)
        nc.scalar.activation(idle[:, 3:4], idle[:, 2:3], ACT.Exp).then_inc(exped, 2)
        FIRST = 0
        weights_hi(0, 0)
        for b in range(2):
            queries_hi(FIRST, b)
        tiles_hi(0, range(N_G))
        weights_hi(0, 1)
        in_turn(act, unit)

    @block.vector
    def _(dve):
        def tiles_lo(v, js):
            for j in js:
                dve.wait_ge(g_hi_done, v * N_G + (j + 1))
                nc.vector.tensor_tensor(g_lo[g_at(j)], by_batch(scores[:, j % 4, 0:GK]),
                                        g_hi[g_at(j)].bitcast(F32), ALU.subtract).then_inc(g_lo_done, 1)

        def tiles_uT(u, js):
            for j in js:
                dve.wait_ge(uT_made, u * N_G + (j + 1))
                nc.vector.tensor_copy(uT[g_at(j)], by_batch(work[:, j % 4, 0:GK])).then_inc(uT_dve, 1)

        def maxima(u, i):
            k = i % 2
            dve.wait_ge(scored, u * ITEMS + (i + 1))
            nc.vector.tensor_reduce(neg_max[k][:].rearrange("p (a h) -> p a h", a=2),
                                    scores[:, 2 * k:2 * k + 2, 0:HFLAT].rearrange("p a (h n) -> p a h n", n=SK),
                                    AX.X, ALU.max, negate=True).then_inc(maxed, 1)

        def pairs_lo(u, pairs):
            for s in pairs:
                _, r, at = u_pair(s)
                dve.wait_ge(u_hi_done, u * N_U + (s + 1))
                nc.vector.tensor_tensor(u_lo[at], work[0:r, bank(s), :].rearrange("p (a n) -> p a n", a=2),
                                        u_hi[at].bitcast(F32), ALU.subtract).then_inc(u_lo_done, 1)

        def totals(u, i):
            k = i % 3
            dve.wait_ge(exped, u * ITEMS + (i + 3))
            nc.vector.tensor_reduce(total[k][:], probs[k][:].rearrange("p (h n) -> p h n", n=SK),
                                    AX.X, ALU.add).then_inc(totalled, 1)
            dve.wait_ge(totalled, u * ITEMS + (i + 1))
            nc.vector.reciprocal(recip[k][:], total[k][:]).then_inc(recips, 1)

        def turned_lo(u, i):
            dve.wait_ge(pT_hi_done, u * ITEMS + (i + 1))
            q = slice(i % QT * P, (i % QT + 1) * P)
            hi, lo = pT_hi[i // QT % 2], pT_lo[i // QT % 2]
            nc.vector.tensor_tensor(lo[:, 0:FT - 1, q], work[:, 0, :].rearrange("p (t q) -> p t q", q=P),
                                    hi[:, 0:FT - 1, q].bitcast(F32), ALU.subtract)
            nc.vector.tensor_tensor(lo[0:LAST, FT - 1, q], work[0:LAST, 1, 0:P],
                                    hi[0:LAST, FT - 1, q].bitcast(F32), ALU.subtract).then_inc(pT_lo_done, 1)

        def result(u, lh, b):
            k = b % 2
            dve.wait_ge(attended, u * GB + (b + 1))
            dve.wait_ge(base_in[k], u * 32 + 16 * (b // 2 + 1))
            dve.wait_ge(stored[(b + 2) % GB], u * 32 + 32 * (1 + b // 2))
            for c in range(CT):
                last = nc.vector.scalar_tensor_tensor(
                    res[k][:, c, :], work[:, 2 + k, c * SQ:(c + 1) * SQ], bo_sb[:, lh, c:c + 1],
                    base[k][:, c, :], ALU.add, ALU.add)
            last.then_inc(res_done, 1)

        def split_lo(lh, m):
            dve.wait_ge(wh_hi_done[m], lh + 1)
            nc.vector.tensor_tensor(wh_lo[m][:], wh_lo[m][:].bitcast(F32), wh_hi[m][:].bitcast(F32),
                                    ALU.subtract).then_inc(wh_split[m], 1)

        def unit(u, lh, weights):
            maxima(u, 0)
            maxima(u, 1)
            tiles_uT(u, range(1, N_G // 2, 2))
            totals(u, 0)
            maxima(u, 2)
            tiles_uT(u, range(N_G // 2 + 1, N_G, 2))
            pairs_lo(u, range(N_U - 3))
            totals(u, 1)
            pairs_lo(u, [N_U - 3])
            turned_lo(u, 0)
            maxima(u, 3)
            totals(u, 2)
            pairs_lo(u, [N_U - 2])
            turned_lo(u, 1)
            pairs_lo(u, [N_U - 1])
            another = u is not LAST_UNIT
            for i in range(2, ITEMS - 2):
                maxima(u, i + 2)
                if i == 2:
                    totals(u, 3)
                turned_lo(u, i)
                if i in (3, 5):
                    result(u, lh, i // 2 - 1)
                totals(u, i + 2)
                if weights and i in (3, 4):
                    split_lo(lh + 1, i - 3)
            if another:
                tiles_lo(u + 1, G_PARTS[0])
            turned_lo(u, ITEMS - 2)
            if another:
                tiles_lo(u + 1, G_PARTS[1])
            turned_lo(u, ITEMS - 1)
            if another:
                tiles_lo(u + 1, G_PARTS[2])
            result(u, lh, GB - 2)
            if another:
                tiles_lo(u + 1, G_PARTS[3])
                tiles_lo(u + 1, G_PARTS[4])
            result(u, lh, GB - 1)

        nc.vector.memset(idle[:, 2:3], 0.0).then_inc(zeroed, 1)
        for m in range(2):
            nc.vector.memset(kv[m][:].bitcast(F32), 0.0).then_inc(zeroed, 1)
        nc.vector.memset(idle[:, 0:1], 0.0).then_inc(pT_lo_done, 1)
        nc.vector.memset(idle[:, 1:2], 0.0).then_inc(res_done, 2)
        split_lo(0, 0)
        tiles_lo(0, range(N_G))
        split_lo(0, 1)
        in_turn(dve, unit)

    @block.gpsimd
    def _(pool):
        def queries_lo(v, b):
            k = b % 2
            pool.wait_ge(x_hi_done, v * GB + (b + 1))
            nc.gpsimd.tensor_tensor(x_lo[k][:], xq[k][:], x_hi[k][:].bitcast(F32), ALU.subtract).then_inc(x_split, 1)

        def unit(u):
            for i in range(ITEMS):
                k = i % 3
                pool.wait_ge(recips, u * ITEMS + (i + 1))
                p3 = probs[k][:].rearrange("p (h n) -> p h n", n=SK)
                nc.gpsimd.tensor_tensor(p3, p3, recip[k][:].unsqueeze(2).to_broadcast((P, HH, SK)),
                                        ALU.mult).then_inc(normed, 1)
                if i in (0, 2):
                    queries_lo(u, i // 2 + 2)
                if i in (5, 7) and u is not LAST_UNIT:
                    queries_lo(u + 1, i // 2 - 2)

        for b in range(2):
            queries_lo(0, b)
        with pool.Fori(0, LAST_UNIT) as u:
            unit(u)
        unit(LAST_UNIT)

    @block.tensor
    def _(pe):
        def products(out, m, h, c):
            for n, w in enumerate((wh_hi, wh_lo)):
                last = nc.tensor.matmul(out, w[m][:, h, c * P:(c + 1) * P], kv[m][:, h, :],
                                        start=(n == 0), stop=(n == 1))
            return last

        def make_g(v, lh, js):
            for j in js:
                if j == 0:
                    pe.wait_ge(kv_in[0], v * 32 + 32)
                    pe.wait_ge(wh_split[0], lh + 1)
                if v is not FIRST and j in (0, 2):
                    pe.wait_ge(exped, v * ITEMS + (1 + j // 2))
                if j >= 4:
                    pe.wait_ge(g_lo_done, v * N_G + (j - 3))
                products(scores[:, j % 4, 0:GK], 0, j // CT, j % CT).then_inc(g_made, 1)

        def make_uT(u, lh, js):
            for j in js:
                if j == 0:
                    pe.wait_ge(kv_in[1], u * 32 + 32)
                    pe.wait_ge(wh_split[1], lh + 1)
                    pe.wait_ge(pT_lo_done, u * ITEMS + 1)
                if j in (2, 3):
                    pe.wait_ge(res_done, u * GB + (j - 1))
                if j >= 4:
                    pe.wait_ge(uT_dve if j % 2 else uT_act, u * (N_G // 2) + (j - 4) // 2 + 1)
                products(work[:, j % 4, 0:GK], 1, j // CT, j % CT).then_inc(uT_made, 1)

        def make_u(u, pairs):
            for s in pairs:
                tiles, r, _ = u_pair(s)
                if s < 4:
                    pe.wait_ge(uT_dve if s % 2 else uT_act, u * (N_G // 2) + ((N_G - 4 + s) // 2 + 1))
                else:
                    pe.wait_ge(u_lo_done, u * N_U + (s - 3 if s < N_U - 2 else s - 1))
                for k, (b, t) in enumerate(tiles):
                    for c in range(CT):
                        last = nc.tensor.transpose(work[0:r, bank(s), (k * CT + c) * P:(k * CT + c + 1) * P],
                                                   uT[:, c, b, t * P:t * P + r], ident[:])
                last.then_inc(u_made, 1)

        def score(u, lh, i):
            b, q, k = i // QT, slice(i % QT * P, (i % QT + 1) * P), i % 2
            if i == 0:
                pe.wait_ge(g_lo_done, u * N_G + N_G)
            pe.wait_ge(x_split, u * GB + (b + 1))
            pe.wait_ge(exped, u * ITEMS + (i + 1))
            x = (x_hi[b % 2], x_lo[b % 2])
            out = [scores[:, 2 * k + a, 0:HFLAT] for a in range(2)]
            for c in range(CT):
                for n, (xp, gp) in enumerate(((x[0], g_hi), (x[0], g_lo), (x[1], g_hi))):
                    for a in range(2):
                        nc.tensor.matmul(out[a], xp[:, c, q], gp[:, c, b, a * HFLAT:(a + 1) * HFLAT],
                                         start=(c == 0 and n == 0), stop=False)
            for a in range(2):
                last = nc.tensor.matmul(out[a], penalty[:, q], key_is[:, lh // 2, :], start=False, stop=True)
            last.then_inc(scored, 1)

        def turn(u, i):
            if i == 0:
                pe.wait_ge(u_lo_done, u * N_U + (N_U - 4))
            pe.wait_ge(normed, u * ITEMS + (i + 1))
            pe.wait_ge(pT_lo_done, u * ITEMS + (i + 1))
            for t in range(FT):
                n = rows_of(t)
                out = work[:, 0, t * P:(t + 1) * P] if t < FT - 1 else work[0:n, 1, 0:P]
                last = nc.tensor.transpose(out, probs[i % 3][:, t * P:t * P + n], ident[:])
            last.then_inc(turned, 1)

        def attend_values(u, b, cs=range(CT)):
            if b == 0:
                pe.wait_ge(u_lo_done, u * N_U + N_U)
            if 0 in cs:
                pe.wait_ge(pT_lo_done, u * ITEMS + (2 * b + 3))
                pe.wait_ge(res_done, u * GB + (b + 1))
            for c in cs:
                for t in range(FT):
                    r = rows_of(t)
                    for n, (up, pp) in enumerate(((u_hi, pT_hi[b % 2]), (u_hi, pT_lo[b % 2]), (u_lo, pT_hi[b % 2]))):
                        last = nc.tensor.matmul(work[:, 2 + b % 2, c * SQ:(c + 1) * SQ],
                                                up[0:r, b, t, c * P:(c + 1) * P], pp[0:r, t, :],
                                                start=(t == 0 and n == 0), stop=(t == FT - 1 and n == 2))
            if CT - 1 in cs:
                last.then_inc(attended, 1)

        def unit(u, lh, weights):
            score(u, lh, 0)
            score(u, lh, 1)
            make_uT(u, lh, range(N_G // 2))
            score(u, lh, 2)
            make_uT(u, lh, range(N_G // 2, N_G))
            make_u(u, range(N_U - 2))
            for i in range(ITEMS - 2):
                if i:
                    score(u, lh, i + 2)
                if i == 1:
                    make_u(u, range(N_U - 2, N_U))
                turn(u, i)
                if i >= 2:
                    attend_values(u, i // 2 - 1, [i % 2])

            def next_g(part):
                if u is not LAST_UNIT:
                    make_g(u + 1, lh + 1 if weights else lh, G_PARTS[part])
            next_g(0)
            turn(u, ITEMS - 2)
            attend_values(u, GB - 2, [0])
            next_g(1)
            turn(u, ITEMS - 1)
            next_g(2)
            attend_values(u, GB - 2, [1])
            next_g(3)
            attend_values(u, GB - 1, [0])
            next_g(4)
            attend_values(u, GB - 1, [1])

        nc.tensor.transpose(work[:, 0, 0:P], ident[:], ident[:]).then_inc(turned, 2)
        FIRST = 0
        make_g(FIRST, 0, range(N_G))
        in_turn(pe, unit)


def kernel(**inputs):
    import numpy as np
    import concourse.bacc as bacc
    from concourse.bass_utils import run_bass_kernel_spmd

    a = {k: np.asarray(v) for k, v in inputs.items()}
    L = [f"L{l}_xattn_" for l in range(LAYERS)]

    def heads_first(w, d):
        out = np.zeros((2, HD, HH, C), np.float32)
        out[:, :d] = w.reshape(2, HH, d, C).transpose(0, 2, 1, 3)
        return out.reshape(2, HD, HH * C)

    wheads = np.zeros((HALVES, 2, HD, HH * C), np.float32)
    bo = np.zeros((P, HALVES, CT), np.float32)
    for l in range(LAYERS):
        q, o, d = ("wq", "wo", HD0) if l == 0 else ("Wq", "Wo", HD)
        wheads[2 * l:2 * l + 2, 0] = heads_first(a[L[l] + q].T, d)
        wheads[2 * l:2 * l + 2, 1] = heads_first(a[L[l] + o], d)
        if l:
            bo[:, 2 * l, :] = a[L[l] + "bo"].reshape(CT, P).T
    arrays = {
        "xT": a["x"].reshape(B * SQ, C).T,
        "ctxT": a["ctx_2048"].reshape(B * SK, E).T,
        "wkv0": np.concatenate([a[L[0] + "wk"], a[L[0] + "wv"]], axis=1),
        "wkv": np.stack([a[L[l] + w] for l in range(1, LAYERS) for w in ("Wk", "Wv")]),
        "wheads": wheads,
        "normw": a[L[0] + "norm_w"].reshape(CT, P).T,
        "bo": bo.reshape(P, HALVES * CT),
        "masks": np.stack([a["mask_S_fk1"], a["mask_S_fk0"]]),
        "tokens": np.concatenate([a[L[l] + f"token_indices_{s}"] for l in range(1, LAYERS) for s in "AB"])[None, :],
    }
    arrays = {k: np.ascontiguousarray(v) for k, v in arrays.items()}
    nc = bacc.Bacc("TRN2", target_bir_lowering=False, num_devices=1)
    aps = {k: nc.dram_tensor(k, v.shape, mybir.dt.from_np(v.dtype), kind="ExternalInput").ap()
           for k, v in arrays.items()}
    outT = nc.dram_tensor("outT", (C, B * SQ), F32, kind="ExternalOutput").ap()
    build(nc, outT=outT, **aps)
    r = run_bass_kernel_spmd(nc, [arrays], core_ids=[0])
    return np.ascontiguousarray(r.results[0]["outT"].T).reshape(B, SQ, C)
```
